# Optimizing a Trainium2 kernel written in Bass

```python
import numpy as np
import jax
import jax.numpy as jnp

def _softmax(x, axis=-1):
    return jax.nn.softmax(x, axis=axis)

def _gelu(x):
    return jax.nn.gelu(x, approximate=True)

def _silu(x):
    return jax.nn.silu(x)

def _sigmoid(x):
    return jax.nn.sigmoid(x)

def _layernorm(x, axis=-1, eps=1e-05):
    m = jnp.mean(x, axis=axis, keepdims=True)
    v = jnp.var(x, axis=axis, keepdims=True)
    return (x - m) / jnp.sqrt(v + eps)

def _scatter_add(tgt, idx, src, axis=0):
    return tgt.at[idx].add(src)

def _segment_sum(src, seg, n):
    return jax.ops.segment_sum(src, seg, n)
kernel_name = 'mk_adaln_attn_ffn_d1_seqx_r8_8c3dda'

def setup_inputs(seed: int=0):
    np.random.seed(seed)
    _w = jnp.asarray

    def _rec_inputs():
        import jax
        import jax.numpy as jnp
        _rk = jax.random.key(seed)
        x = 7.22e-05 + 1 * jax.random.normal(jax.random.fold_in(_rk, 1), (8, 256, 128), jnp.float32)
        _lenS = 256 - jax.random.randint(jax.random.fold_in(_rk, 7), (8,), 0, max(1, 256 // 4) + 1, jnp.int32)
        _lenS2 = 256 - jax.random.randint(jax.random.fold_in(_rk, 8), (8,), 0, max(1, 256 // 4) + 1, jnp.int32)
        cond_8 = -0.104238 + 1.01173 * jax.random.normal(jax.random.fold_in(_rk, 11), (8, 8), jnp.float32)
        return (x, cond_8)
    x, cond_8 = _rec_inputs()

    def _L0_cond_setup():
        import jax, jax.numpy as jnp
        import numpy as np
        TOP_K = 2
        NUM_MOE_LAYERS = 12

        def _gemma_mlp(x, gate_w, up_w, down_w):
            g = jnp.einsum('bsh,hi->bsi', x, gate_w)
            u = jnp.einsum('bsh,hi->bsi', x, up_w)
            return jnp.einsum('bsi,ih->bsh', jax.nn.gelu(g, approximate=True) * u, down_w)
        key = jax.random.key(seed)
        ks = jax.random.split(key, 8)
        B, S, H, I, E = (32, 32, 128, 512, 8)
        std = 0.02
        return {'x': jax.random.normal(ks[0], (B, S, H), jnp.float32), 'router_logits': jax.random.normal(ks[1], (B, E), jnp.float32), 'skill_gate': jax.random.normal(ks[2], (E, H, I), jnp.float32) * std, 'skill_up': jax.random.normal(ks[3], (E, H, I), jnp.float32) * std, 'skill_down': jax.random.normal(ks[4], (E, I, H), jnp.float32) * std, 'shared_gate': jax.random.normal(ks[5], (H, I), jnp.float32) * std, 'shared_up': jax.random.normal(ks[6], (H, I), jnp.float32) * std, 'shared_down': jax.random.normal(ks[7], (I, H), jnp.float32) * std}
    _L0_cond_all = _L0_cond_setup()
    _L0_cond_in = {k: v for k, v in _L0_cond_all.items() if k in ('skill_gate', 'skill_up', 'skill_down', 'shared_gate', 'shared_up', 'shared_down')}
    del _L0_cond_all

    def _L0_attn_setup():
        import jax, jax.numpy as jnp
        import numpy as np
        D_MODEL = 128
        N_HEADS = 16
        D_LATENT = 32
        HEAD_DIM = D_MODEL // N_HEADS

        def apply_rope(x):
            B, T, H, D = x.shape
            inv_freq = 1.0 / 10000.0 ** (jnp.arange(0, D, 2, dtype=jnp.float32) / D)
            t = jnp.arange(T, dtype=jnp.float32)
            freqs = t[:, None] * inv_freq[None, :]
            sin_f = jnp.sin(freqs)[None, :, None, :]
            cos_f = jnp.cos(freqs)[None, :, None, :]
            x1, x2 = jnp.split(x, 2, axis=-1)
            return jnp.concatenate([x1 * cos_f - x2 * sin_f, x1 * sin_f + x2 * cos_f], axis=-1)
        key = jax.random.key(seed)
        ks = jax.random.split(key, 10)
        B, T = (4, 512)
        s = lambda fan_in: 1.0 / np.sqrt(fan_in)
        return {'x': jax.random.normal(ks[0], (B, T, D_MODEL), dtype=jnp.float32), 'Wq': jax.random.normal(ks[1], (D_MODEL, D_MODEL), dtype=jnp.float32) * s(D_MODEL), 'bq': jnp.zeros((D_MODEL,), jnp.float32), 'Wdown': jax.random.normal(ks[2], (D_MODEL, D_LATENT), dtype=jnp.float32) * s(D_MODEL), 'bdown': jnp.zeros((D_LATENT,), jnp.float32), 'Wup': jax.random.normal(ks[3], (D_LATENT, 2 * D_MODEL), dtype=jnp.float32) * s(D_LATENT), 'bup': jnp.zeros((2 * D_MODEL,), jnp.float32), 'Wout': jax.random.normal(ks[4], (D_MODEL, D_MODEL), dtype=jnp.float32) * s(D_MODEL), 'bout': jnp.zeros((D_MODEL,), jnp.float32)}
    _L0_attn_all = _L0_attn_setup()
    _L0_attn_in = {k: v for k, v in _L0_attn_all.items() if k in ('Wq', 'bq', 'Wdown', 'bdown', 'Wup', 'bup', 'Wout', 'bout')}
    del _L0_attn_all

    def _L0_cond2_setup():
        import jax, jax.numpy as jnp
        import numpy as np
        R = 16
        ALPHA = 32.0
        SCALING = ALPHA / R
        key = jax.random.key(seed)
        ks = jax.random.split(key, 6)
        B, T, C, O, E = (16, 1500, 128, 128, 8)
        x = jax.random.normal(ks[0], (B, T, C), dtype=jnp.float32)
        w = jax.random.uniform(ks[1], (B, E), dtype=jnp.float32)
        W_base = jax.random.normal(ks[2], (O, C), dtype=jnp.float32) * 0.02
        b_base = jax.random.normal(ks[3], (O,), dtype=jnp.float32) * 0.02
        As = jax.random.normal(ks[4], (E, R, C), dtype=jnp.float32) * 0.02
        Bs = jax.random.normal(ks[5], (E, O, R), dtype=jnp.float32) * 0.02
        return {'x': x, 'w': w, 'W_base': W_base, 'b_base': b_base, 'As': As, 'Bs': Bs}
    _L0_cond2_all = _L0_cond2_setup()
    _L0_cond2_in = {k: v for k, v in _L0_cond2_all.items() if k in ('W_base', 'b_base', 'As', 'Bs')}
    del _L0_cond2_all

    def _L0_ffn_setup():
        import jax, jax.numpy as jnp
        import numpy as np
        B, S, D = (4, 256, 128)
        E, F = (8, 512)
        key = jax.random.key(seed)
        ks = jax.random.split(key, 5)
        x = jax.random.normal(ks[0], (B, S, D), dtype=jnp.float32)
        switch_w = jax.random.normal(ks[1], (D, E), dtype=jnp.float32) * D ** (-0.5)
        switch_b = jnp.zeros((E,), dtype=jnp.float32)
        w1 = jax.random.normal(ks[2], (E, D, F), dtype=jnp.float32) * D ** (-0.5)
        b1 = jnp.zeros((E, F), dtype=jnp.float32)
        w2 = jax.random.normal(ks[3], (E, F, D), dtype=jnp.float32) * F ** (-0.5)
        b2 = jnp.zeros((E, D), dtype=jnp.float32)
        return {'x': x, 'switch_w': switch_w, 'switch_b': switch_b, 'w1': w1, 'b1': b1, 'w2': w2, 'b2': b2}
    _L0_ffn_all = _L0_ffn_setup()
    _L0_ffn_in = {k: v for k, v in _L0_ffn_all.items() if k in ('switch_w', 'switch_b', 'w1', 'b1', 'w2', 'b2')}
    del _L0_ffn_all
    return {'x': x, 'cond_8': cond_8, 'L0_cond_skill_gate': _L0_cond_in['skill_gate'], 'L0_cond_skill_up': _L0_cond_in['skill_up'], 'L0_cond_skill_down': _L0_cond_in['skill_down'], 'L0_cond_shared_gate': _L0_cond_in['shared_gate'], 'L0_cond_shared_up': _L0_cond_in['shared_up'], 'L0_cond_shared_down': _L0_cond_in['shared_down'], 'L0_attn_Wq': _L0_attn_in['Wq'], 'L0_attn_bq': _L0_attn_in['bq'], 'L0_attn_Wdown': _L0_attn_in['Wdown'], 'L0_attn_bdown': _L0_attn_in['bdown'], 'L0_attn_Wup': _L0_attn_in['Wup'], 'L0_attn_bup': _L0_attn_in['bup'], 'L0_attn_Wout': _L0_attn_in['Wout'], 'L0_attn_bout': _L0_attn_in['bout'], 'L0_cond2_W_base': _L0_cond2_in['W_base'], 'L0_cond2_b_base': _L0_cond2_in['b_base'], 'L0_cond2_As': _L0_cond2_in['As'], 'L0_cond2_Bs': _L0_cond2_in['Bs'], 'L0_ffn_switch_w': _L0_ffn_in['switch_w'], 'L0_ffn_switch_b': _L0_ffn_in['switch_b'], 'L0_ffn_w1': _L0_ffn_in['w1'], 'L0_ffn_b1': _L0_ffn_in['b1'], 'L0_ffn_w2': _L0_ffn_in['w2'], 'L0_ffn_b2': _L0_ffn_in['b2']}

def reference(x, cond_8, L0_cond_skill_gate, L0_cond_skill_up, L0_cond_skill_down, L0_cond_shared_gate, L0_cond_shared_up, L0_cond_shared_down, L0_attn_Wq, L0_attn_bq, L0_attn_Wdown, L0_attn_bdown, L0_attn_Wup, L0_attn_bup, L0_attn_Wout, L0_attn_bout, L0_cond2_W_base, L0_cond2_b_base, L0_cond2_As, L0_cond2_Bs, L0_ffn_switch_w, L0_ffn_switch_b, L0_ffn_w1, L0_ffn_b1, L0_ffn_w2, L0_ffn_b2):
    import jax
    import jax.numpy as jnp

    def _L0_cond_ref(x, router_logits, skill_gate, skill_up, skill_down, shared_gate, shared_up, shared_down):
        import jax, jax.numpy as jnp
        import numpy as np
        TOP_K = 2
        NUM_MOE_LAYERS = 12

        def _gemma_mlp(x, gate_w, up_w, down_w):
            g = jnp.einsum('bsh,hi->bsi', x, gate_w)
            u = jnp.einsum('bsh,hi->bsi', x, up_w)
            return jnp.einsum('bsi,ih->bsh', jax.nn.gelu(g, approximate=True) * u, down_w)
        B = x.shape[0]
        E = skill_gate.shape[0]
        rw = jax.nn.softmax(router_logits.astype(jnp.float32), axis=-1)
        w, sel = jax.lax.top_k(rw, TOP_K)
        w = w / w.sum(axis=-1, keepdims=True)
        w = w.astype(x.dtype)
        scale = 1.0 / NUM_MOE_LAYERS
        w = scale * w + (1.0 - scale) * jax.lax.stop_gradient(w)
        dense_w = jnp.zeros((B, E), x.dtype).at[jnp.arange(B)[:, None], sel].add(w)

        def step(acc, params):
            g, u, d, we = params
            return (acc + we[:, None, None] * _gemma_mlp(x, g, u, d), None)
        out, _ = jax.lax.scan(step, jnp.zeros_like(x), (skill_gate, skill_up, skill_down, dense_w.T))
        out = out + _gemma_mlp(x, shared_gate, shared_up, shared_down)
        return out

    def _L0_attn_ref(x, Wq, bq, Wdown, bdown, Wup, bup, Wout, bout):
        import jax, jax.numpy as jnp
        import numpy as np
        D_MODEL = 128
        N_HEADS = 16
        D_LATENT = 32
        HEAD_DIM = D_MODEL // N_HEADS

        def apply_rope(x):
            B, T, H, D = x.shape
            inv_freq = 1.0 / 10000.0 ** (jnp.arange(0, D, 2, dtype=jnp.float32) / D)
            t = jnp.arange(T, dtype=jnp.float32)
            freqs = t[:, None] * inv_freq[None, :]
            sin_f = jnp.sin(freqs)[None, :, None, :]
            cos_f = jnp.cos(freqs)[None, :, None, :]
            x1, x2 = jnp.split(x, 2, axis=-1)
            return jnp.concatenate([x1 * cos_f - x2 * sin_f, x1 * sin_f + x2 * cos_f], axis=-1)
        B, T, D = x.shape
        H, Dh = (N_HEADS, HEAD_DIM)
        q = x @ Wq + bq
        kv_latent = x @ Wdown + bdown
        kv = kv_latent @ Wup + bup
        q = q.reshape(B, T, H, Dh)
        kv = kv.reshape(B, T, H, 2 * Dh)
        k, v = jnp.split(kv, 2, axis=-1)
        q = apply_rope(q)
        k = apply_rope(k)
        att = jnp.einsum('bthd,btgd->bthg', q, k) / jnp.sqrt(jnp.float32(Dh))
        att = jax.nn.softmax(att, axis=-1)
        out = jnp.einsum('bthg,btgd->bthd', att, v)
        out = out.reshape(B, T, D)
        return out @ Wout + bout

    def _L0_cond2_ref(x, w, W_base, b_base, As, Bs):
        import jax, jax.numpy as jnp
        import numpy as np
        R = 16
        ALPHA = 32.0
        SCALING = ALPHA / R
        out = jnp.einsum('btc,oc->bto', x, W_base) + b_base
        h = jnp.einsum('btc,erc->bter', x, As)
        lora = jnp.einsum('bter,eor,be->bto', h, Bs, w)
        return out + lora * SCALING

    def _L0_ffn_ref(x, switch_w, switch_b, w1, b1, w2, b2):
        import jax, jax.numpy as jnp
        import numpy as np
        B, S, D = (4, 256, 128)
        E, F = (8, 512)
        b, s, d = x.shape
        t = x.reshape(-1, d)
        logits = t @ switch_w + switch_b
        route_prob = jax.nn.softmax(logits, axis=-1)
        route_prob_max = jnp.max(route_prob, axis=-1)
        routes = jnp.argmax(route_prob, axis=-1)
        out = jnp.zeros_like(t)
        n_experts = w1.shape[0]
        for e in range(n_experts):
            h = jax.nn.gelu(t @ w1[e] + b1[e])
            y = h @ w2[e] + b2[e]
            mask = (routes == e)[:, None]
            out = jnp.where(mask, y, out)
        out = out * route_prob_max[:, None]
        return out.reshape(b, s, d)
    x = x + _L0_attn_ref(_L0_cond_ref(x, cond_8, L0_cond_skill_gate, L0_cond_skill_up, L0_cond_skill_down, L0_cond_shared_gate, L0_cond_shared_up, L0_cond_shared_down), L0_attn_Wq, L0_attn_bq, L0_attn_Wdown, L0_attn_bdown, L0_attn_Wup, L0_attn_bup, L0_attn_Wout, L0_attn_bout)
    x = x + _L0_ffn_ref(_L0_cond2_ref(x, cond_8, L0_cond2_W_base, L0_cond2_b_base, L0_cond2_As, L0_cond2_Bs), L0_ffn_switch_w, L0_ffn_switch_b, L0_ffn_w1, L0_ffn_b1, L0_ffn_w2, L0_ffn_b2)
    return x

_drawn_inputs = setup_inputs


def setup_inputs(seed=0):
    import zlib

    import numpy as np

    out = dict(_drawn_inputs(seed))
    spreads = {'L0_attn_bq': (0.0, 0.8),
     'L0_attn_bdown': (0.0, 0.286),
     'L0_attn_bup': (0.0, 0.325),
     'L0_attn_bout': (0.0, 0.54),
     'L0_ffn_switch_b': (0.0, 1.208),
     'L0_ffn_b1': (0.0, 2.0),
     'L0_ffn_b2': (0.0, 2.0)}
    factors = {'cond_8': 2.702,
     'L0_cond_skill_gate': 8.0,
     'L0_cond_skill_up': 8.0,
     'L0_cond_skill_down': 8.0,
     'L0_cond_shared_gate': 8.0,
     'L0_cond_shared_up': 8.0,
     'L0_cond_shared_down': 8.0,
     'L0_attn_Wq': 8.0,
     'L0_attn_Wdown': 8.0,
     'L0_cond2_b_base': 28.834,
     'L0_cond2_As': 2.696,
     'L0_cond2_Bs': 2.768}
    for name, (base, spread) in spreads.items():
        noise = np.random.default_rng([zlib.crc32(name.encode()), seed]).standard_normal(out[name].shape)
        drawn = base * np.exp(spread * noise) if base else spread * noise
        out[name] = jnp.asarray(drawn.astype(out[name].dtype))
    for name, factor in factors.items():
        out[name] = (out[name] * factor).astype(out[name].dtype)
    return out
```

```python
from contextlib import ExitStack

import concourse.bass as bass
from concourse import mybir

F32 = mybir.dt.float32
F32R = mybir.dt.float32r
BF16 = mybir.dt.bfloat16
U32 = mybir.dt.uint32
I32 = mybir.dt.int32
ACT = mybir.ActivationFunctionType
ALU = mybir.AluOpType
AX = mybir.AxisListType.X

B, S, D = 8, 256, 128
T = B * S
E, F = 8, 512
NH, DH = 16, 8
LAT = 32
TOP_K, MOE_LAYERS = 2, 12
FC = F // 128
TT = T // 128
SLOT_TILES = TT + E - 1
SLOTS = SLOT_TILES * 128
PROB, IDX, ROW = 2 * D, 2 * D + 1, 2 * D + 2
NO_TOKEN = 1 << 20
RING = 4
LEAD = SLOT_TILES % RING + RING
FFN_W = 2 * F + FC + D

FIELDS = [("switch_b", E), ("cond_rows", B), ("wq", D), ("wq_swap", D), ("wk", D), ("wk_swap", D), ("wv", D),
          ("wdown", LAT), ("bdown", 1), ("wout", D), ("bout", 1), ("wbase", D),
          ("bbase", 1), ("lora_a", D), ("lora_b", D), ("switch_w", E), ("cos", 4 * D), ("sin", 4 * D), ("ident", D),
          ("earlier_row", D), ("falling", E), ("ramp", TT), ("before", E * E), ("slot_tile", SLOT_TILES)]
AT, CONST_W = {}, 0
for _name, _width in FIELDS:
    AT[_name] = (CONST_W, _width)
    CONST_W += _width


def adaln_program(nc, x_t, cond, experts, ffn, consts, query_bias, token_ids, out):
    ctx = ExitStack()
    with ctx:
        def sb(name, shape, dt=F32):
            return ctx.enter_context(nc.sbuf_tensor(name, shape, dt))

        def sem(name):
            return ctx.enter_context(nc.semaphore(name))

        gu_bank = [ctx.enter_context(nc.psum_tensor(f"gu_bank{i}", [128, 2, 512], F32)) for i in (0, 1)]
        y_bank, x0, x1, x2 = [ctx.enter_context(nc.psum_tensor(n, [128, 512], F32)) for n in ("y_bank", "x0", "x1", "x2")]

        slot_dram = nc.dram_tensor("slot_dram", [SLOTS, ROW], F32).ap()

        c = sb("c", [128, CONST_W])
        cb = sb("cb", [128, B, E])
        ids = sb("ids", [128, TT], I32)
        xt = sb("xt", [128, T])

        def const(name, rows=128):
            a, w = AT[name]
            return c[0:rows, a:a + w]

        r_max = sb("r_max", [128, B])
        r_exp = sb("r_exp", [128, B, E])
        r_sum = sb("r_sum", [128, B])
        r_prob = sb("r_prob", [128, B, E])
        r_top = sb("r_top", [128, B, 8])
        chosen = sb("chosen", [128, B, 8], U32)
        r_norm = sb("r_norm", [128, B])
        r_w = sb("r_w", [128, B, TOP_K])
        r_part = sb("r_part", [128, B, TOP_K])
        weight = sb("weight", [128, B, TOP_K + 1])

        xt_hi = sb("xt_hi", [128, T], F32R)
        xt_lo = sb("xt_lo", [128, T], F32R)
        gu = [sb(f"gu{k}", [128, 2 * F]) for k in range(3)]
        gu_hi = [sb(f"gu_hi{k}", [128, 2 * F], F32R) for k in range(3)]
        gu_lo = [sb(f"gu_lo{k}", [128, 2 * F], F32R) for k in range(3)]
        down = [sb(f"down{k}", [128, F]) for k in range(3)]
        gelu = sb("gelu", [128, 2, 512])
        hid = sb("hid", [128, 3, 512])

        lora_scaled = sb("lora_scaled", [128, B, D])
        w_eff = sb("w_eff", [128, B, D])
        w_now = sb("w_now", [128, D])
        bias_in_f = sb("bias_in_f", [1, 8 * D])
        bias_rest = sb("bias_rest", [1, 8 * D])
        bias_split = sb("bias_split", [1, 3, 8 * D], BF16)
        bias_rows = sb("bias_rows", [3, 8 * D], BF16)
        y = sb("y", [128, S])
        lat = sb("lat", [LAT + 1, S])
        rope = sb("rope", [128, 2, 4 * D])
        qk = sb("qk", [128, 2, 2, NH, DH])
        qk_prod = sb("qk_prod", [128, 2, NH, NH, DH])
        score = sb("score", [128, 2, NH, NH])
        s_max = sb("s_max", [128, 2, NH])
        prob = sb("prob", [128, 2, NH, NH])
        v = sb("v", [128, 2, DH, NH])
        pv_prod = sb("pv_prod", [128, 2, NH, DH, NH])
        mixed = sb("mixed", [128, 2, NH, DH])
        den = sb("den", [128, 2, NH])
        mixed_tok = sb("mixed_tok", [128, 2, D])
        mixed_t = sb("mixed_t", [128, S])
        x1_t = sb("x1_t", [128, S])
        t_t = sb("t_t", [128, S])
        rows = sb("rows", [128, TT, ROW])
        logit = sb("logit", [128, TT, E])

        l_max = sb("l_max", [128, TT])
        l_exp = sb("l_exp", [128, TT, E])
        l_sum = sb("l_sum", [128, TT])
        l_eq = sb("l_eq", [128, TT, E])
        l_first = sb("l_first", [128, TT])
        onehot = sb("onehot", [128, TT, E])
        onehot_b = sb("onehot_b", [128, TT * E], BF16)
        earlier_b = sb("earlier_b", [128, 128], BF16)
        ones_b = sb("ones_b", [128, 128], BF16)
        total = sb("total", [128, TT, E])
        scan = [sb(f"scan{i}", [128, TT, E]) for i in (0, 1)]
        over = sb("over", [128, E, TT])
        n_tiles = sb("n_tiles", [128, E])
        prev_tiles = sb("prev_tiles", [128, E, E])
        first_tile = sb("first_tile", [128, E])
        end_tile = sb("end_tile", [128, E])
        place = sb("place", [128, TT, E])
        slot_f = sb("slot_f", [128, TT])
        slot = sb("slot", [128, TT], U32)
        ended = sb("ended", [128, SLOT_TILES, E])
        owner_f = sb("owner_f", [128, SLOT_TILES])
        owner = sb("owner", [128, SLOT_TILES], U32)
        empty = sb("empty", [128, ROW])

        fw = [sb(f"fw{i}", [128, FFN_W]) for i in (0, 1)]
        srow = [pv_prod[:].rearrange("p a b c d -> p (a b c d)")[:, i * ROW:(i + 1) * ROW] for i in range(RING)]
        st = [hid[:, 2, i * 128:(i + 1) * 128] for i in (0, 1)]
        fh = [gelu[:, i, :].rearrange("p (k s) -> p k s", k=FC) for i in (0, 1)]
        y1 = sb("y1", [128, D])
        z = [hid[:, i, 0:D] for i in (0, 1)]
        yo = [sb(f"yo{i}", [128, D]) for i in (0, 1)]

        cond_in, x_in, const_in, ids_in = sem("cond_in"), sem("x_in"), sem("const_in"), sem("ids_in")
        gu_in = [sem(f"gu_in{k}") for k in range(3)]
        down_in = [sem(f"down_in{k}") for k in range(3)]
        empty_out = sem("empty_out")
        rt, r_expd, chosen_done, weight_done = sem("rt"), sem("r_expd"), sem("chosen_done"), sem("weight_done")
        x_hi_done, x_lo_done = sem("x_hi_done"), sem("x_lo_done")
        gu_hi_done = [sem(f"gu_hi_done{k}") for k in range(3)]
        gu_lo_done = [sem(f"gu_lo_done{k}") for k in range(3)]
        slot_used = [sem(f"slot_used{k}") for k in range(3)]
        gu_mm, gelu_done, hid_done, down_mm = (
            sem(n) for n in ("gu_mm", "gelu_done", "hid_done", "down_mm"))
        lora_done, eff_mm, eff_done, w_now_done = sem("lora_done"), sem("eff_mm"), sem("eff_done"), sem("w_now_done")
        ones_set, bias_in, bias_done, bias_placed = sem("ones_set"), sem("bias_in"), sem("bias_done"), sem("bias_placed")
        names = ("y_read lat_mm lat_read q_mm k_mm v_mm v_read rope_read turned qk_prod_done score_done max_done sub_done "
                 "exp_done pv_prod_done pv_done sum_done recip_done tok_done tokt_mm tokt_read x1_mm x1_made t_mm t_read "
                 "row_mm row_read logit_mm logit_read")
        s = {n: sem(n) for n in names.split()}
        (rr, rr_exp, count_mm, rr_slot, rr_owner, rr_cols, scattered, st_mm, st_done, h_mm, h_done, fy_mm,
         y1_done, z_done, yo_done) = (
            sem(n) for n in ("rr", "rr_exp", "count_mm", "rr_slot", "rr_owner", "rr_cols", "scattered",
                             "st_mm", "st_done", "h_mm", "h_done", "fy_mm", "y1_done", "z_done", "yo_done"))
        w_in = [sem(f"w_in{i}") for i in (0, 1)]
        row_in, stored = ([sem(f"{n}{i}") for i in range(RING)] for n in ("row_in", "stored"))

        def wait(eng, semaphore, value):
            if not (isinstance(value, int) and value <= 0):
                eng.wait_ge(semaphore, value)

        def loads(t, q, ring):
            return (16 // ring) * (t - q) + 16

        def tiles(eng, lead, end, body):
            for t in range(lead):
                body(t, t % RING)
            with eng.Fori(0, (end - lead) // RING) as i:
                for j in range(RING):
                    body(RING * i + lead + j, (lead + j) % RING)

        def pipeline(eng, step):
            for n in range(3):
                step(n)
            with eng.Fori(3, B) as n:
                step(n)
            for n in range(B, B + 3):
                step(n)

        def has(n, lag):
            return not isinstance(n, int) or 0 <= n - lag < B

        UNITS = [(k, half) for k in (2, 0, 1) for half in (0, 1)]
        NU = len(UNITS)

        def used_by(b, k):
            return (b - 1) * NU + UNITS.index((k, 1)) + 1 if not (isinstance(b, int) and b == 0) else 0

        g_bank = [gu_bank[i][:, 0, :] for i in (0, 1)]
        u_bank = [gu_bank[i][:, 1, :] for i in (0, 1)]
        h_bank, st_bank, fy_bank = g_bank, [x0, x1], [x2, y_bank]

        block = ctx.enter_context(nc.Block())

        @block.sync
        def _(sp):
            sp.dma_start(cb[:].rearrange("p b e -> p (b e)"), cond).then_inc(cond_in, 16)
            sp.dma_start(xt[:], x_t).then_inc(x_in, 16)
            sp.dma_start(gu[2][:], experts[E, :, 0:2 * F]).then_inc(gu_in[2], 16)
            sp.dma_start(down[2][:], experts[E, :, 2 * F:3 * F]).then_inc(down_in[2], 16)
            sp.wait_ge(chosen_done, 1)

            def expert_load(b, k):
                e = sp.value_load(chosen[0:1, b, k:k + 1] if isinstance(b, int) else
                                  chosen[:].rearrange("p b e -> p (b e)")[0:1, bass.ds(b * 8 + k, 1)],
                                  min_val=0, max_val=E - 1)
                src = experts[bass.ds(e, 1)].rearrange("a p f -> p (a f)")
                wait(sp, gu_hi_done[k], b)
                wait(sp, gu_lo_done[k], b)
                sp.dma_start(gu[k][:], src[:, 0:2 * F]).then_inc(gu_in[k], 16)
                wait(sp, slot_used[k], b)
                sp.dma_start(down[k][:], src[:, 2 * F:3 * F]).then_inc(down_in[k], 16)

            expert_load(0, 0)
            sp.dma_start(c[:], consts).then_inc(const_in, 16)
            sp.dma_start(bias_in_f[:], query_bias).then_inc(bias_in, 16)
            sp.dma_start(ids[:], token_ids).then_inc(ids_in, 16)
            expert_load(0, 1)
            sp.wait_ge(bias_done, 3)
            for i in range(3):
                sp.dma_start(bias_rows[i:i + 1, :], bias_split[:, i, :]).then_inc(bias_placed, 16)
            with sp.Fori(1, B) as b:
                expert_load(b, 0)
                expert_load(b, 1)

            sp.wait_ge(rr_owner, 1)

            def ffn_load(t, q):
                par = q % 2
                e = sp.value_load(owner[0:1, bass.ds(t, 1)], min_val=0, max_val=E - 1)
                wait(sp, z_done, t - 1)
                sp.dma_start(fw[par][:], ffn[bass.ds(e, 1)].rearrange("a p f -> p (a f)")).then_inc(w_in[par], 16)
                if isinstance(t, int) and t == 0:
                    sp.wait_ge(scattered, 16 * TT)
                wait(sp, stored[q], loads(t - RING, q, RING))
                sp.dma_start(srow[q], slot_dram[bass.ds(t * 128, 128), :]).then_inc(row_in[q], 16)

            tiles(sp, LEAD, SLOT_TILES, ffn_load)
            for q in range(RING):
                sp.wait_ge(stored[q], loads(SLOT_TILES - 1 - (SLOT_TILES - 1 - q) % RING, q, RING))

        @block.gpsimd
        def _(pool):
            nc.gpsimd.memset(ones_b[:], 1.0).then_inc(ones_set, 1)
            nc.gpsimd.memset(lat[:], 1.0).then_inc(ones_set, 1)
            nc.gpsimd.memset(empty[:], 0.0).then_inc(ones_set, 1)
            pool.wait_ge(ones_set, 3)
            nc.gpsimd.memset(empty[:, IDX:IDX + 1].bitcast(I32), NO_TOKEN).then_inc(ones_set, 1)
            pool.wait_ge(ones_set, 4)
            for i in range(SLOT_TILES):
                pool.dma_start(slot_dram[i * 128:(i + 1) * 128, :], empty[:]).then_inc(empty_out, 16)

            def low(b, k):
                pool.wait_ge(gu_in[k], 16 * b + 16)
                pool.wait_ge(gu_hi_done[k], b + 1)
                wait(pool, gu_mm, used_by(b, k))
                nc.gpsimd.tensor_tensor(gu_lo[k][:], gu[k][:], gu_hi[k][:].bitcast(F32), ALU.subtract)\
                    .then_inc(gu_lo_done[k], 1)

            low(0, 2)

            def step(n):
                if has(n, 0):
                    low(n, 0)
                for tile in (0, 1):
                    if has(n, 2):
                        pool.wait_ge(s["v_read"], n - 1)
                        wait(pool, s["pv_done"], 2 * (n - 2) + tile - 1 if tile else 2 * (n - 2))
                        pool.wait_ge(s["exp_done"], n - 1)
                        nc.gpsimd.tensor_tensor(pv_prod[:, tile], prob[:, tile].unsqueeze(2).broadcast_to([128, NH, DH, NH]),
                                                v[:, tile].unsqueeze(1).broadcast_to([128, NH, DH, NH]), ALU.mult)\
                            .then_inc(s["pv_prod_done"], 1)
                    if tile == 0 and has(n, 0):
                        low(n, 1)

            pipeline(pool, step)

            pool.wait_ge(empty_out, 16 * SLOT_TILES)
            pool.wait_ge(s["row_read"], B)
            pool.wait_ge(rr_cols, 2)
            pool.wait_ge(rr_slot, 1)
            for i in range(TT):
                pool.indirect_dma_start(slot_dram, bass.IndirectOffsetOnAxis(slot[:, i:i + 1], 0),
                                        rows[:, i, :], None).then_inc(scattered, 16)

            def store(q):
                pool.indirect_dma_start(out, bass.IndirectOffsetOnAxis(srow[q][:, IDX:IDX + 1].bitcast(U32), 0),
                                        yo[q % 2][:], None, bounds_check=T - 1, oob_is_err=False).then_inc(stored[q], 16)

            def add_x1(t, q):
                if not (isinstance(t, int) and t < 2):
                    pool.wait_ge(stored[(q - 2) % RING], loads(t - 2, (q - 2) % RING, RING))
                wait(pool, yo_done, t)
                pool.wait_ge(z_done, t + 1)
                nc.gpsimd.tensor_tensor(yo[q % 2][:], z[q % 2], srow[q][:, D:2 * D], ALU.add).then_inc(yo_done, 1)
                if not (isinstance(t, int) and t == 0):
                    store((q - 1) % RING)

            tiles(pool, LEAD, SLOT_TILES, add_x1)
            pool.wait_ge(yo_done, SLOT_TILES)
            store((SLOT_TILES - 1) % RING)
            for q in range(RING):
                pool.wait_ge(stored[q], loads(SLOT_TILES - 1 - (SLOT_TILES - 1 - q) % RING, q, RING))

        @block.scalar
        def _(act):
            act.wait_ge(rt, 2)
            nc.scalar.activation(r_exp[:], r_exp[:], ACT.Exp).then_inc(r_expd, 1)

            def high(b, k):
                act.wait_ge(gu_in[k], 16 * b + 16)
                wait(act, gu_mm, used_by(b, k))
                nc.scalar.activation(gu_hi[k][:], gu[k][:], ACT.Copy).then_inc(gu_hi_done[k], 1)

            def unit(b, n):
                act.wait_ge(gu_mm, b * NU + n + 1)
                wait(act, hid_done, b * NU + n - 1)
                nc.scalar.activation(gelu[:, n % 2, :], g_bank[n % 2], ACT.Gelu_apprx_tanh).then_inc(gelu_done, 1)

            high(0, 2)
            act.wait_ge(const_in, 16)
            act.wait_ge(ones_set, 4)

            def step(n):
                if has(n, 0):
                    high(n, 0)
                    unit(n, 0)
                    high(n, 1)
                if has(n, 3):
                    wait(act, s["q_mm"], min(n - 1, B) if isinstance(n, int) else n - 1)
                    act.wait_ge(s["t_mm"], n - 2)
                    nc.scalar.activation(t_t[:], x0[:, 0:S], ACT.Identity, bias=const("bbase")).then_inc(s["t_read"], 1)
                if has(n, 0):
                    unit(n, 1)
                if has(n, 1):
                    wait(act, s["q_mm"], n - 1)
                    act.wait_ge(slot_used[1], n)
                    nc.scalar.activation(y[:], y_bank[:, 0:S], ACT.Copy).then_inc(s["y_read"], 1)
                if has(n, 3):
                    act.wait_ge(s["row_mm"], n - 2)
                    dst = rows[:].rearrange("p t r -> p (t r)")[:, bass.ds((n - 3) * 2 * ROW, 2 * ROW)]
                    nc.scalar.activation(dst.rearrange("p (t r) -> p t r", t=2)[:, :, 0:2 * D],
                                         x1[:].rearrange("p (t r) -> p t r", t=2), ACT.Copy).then_inc(s["row_read"], 1)
                if has(n, 0):
                    unit(n, 2)
                if has(n, 1):
                    wait(act, s["v_mm"], n - 1)
                    act.wait_ge(s["lat_mm"], n)
                    nc.scalar.activation(lat[0:LAT, :], x2[0:LAT, 0:S], ACT.Identity, bias=const("bdown", LAT))\
                        .then_inc(s["lat_read"], 1)
                if has(n, 0):
                    unit(n, 3)
                if has(n, 2):
                    act.wait_ge(s["tokt_mm"], n - 1)
                    wait(act, s["x1_mm"], n - 2)
                    nc.scalar.activation(mixed_t[:], x0[:, 0:S], ACT.Copy).then_inc(s["tokt_read"], 1)
                if has(n, 0):
                    unit(n, 4)
                if has(n, 1):
                    wait(act, s["pv_prod_done"], 2 * (n - 1))
                    act.wait_ge(s["v_mm"], n)
                    nc.scalar.activation(v[:].rearrange("p t d g -> p t g d"),
                                         x2[:, 0:2 * D].rearrange("p (t g d) -> p t g d", t=2, d=DH),
                                         ACT.Copy).then_inc(s["v_read"], 1)
                if has(n, 0):
                    unit(n, 5)
                if has(n, 1):
                    act.wait_ge(s["sub_done"], n)
                    nc.scalar.activation(prob[:], score[:], ACT.Exp, scale=float(DH) ** -0.5).then_inc(s["exp_done"], 1)

            pipeline(act, step)

            act.wait_ge(rr, 2)
            nc.scalar.activation(l_exp[:], l_exp[:], ACT.Exp).then_inc(rr_exp, 1)

            def ffn_gelu(t, q):
                par = q % 2
                act.wait_ge(w_in[par], loads(t, par, 2))
                wait(act, fy_mm, t - 1)
                act.wait_ge(h_mm, t + 1)
                for k in range(FC):
                    ins = nc.scalar.activation(fh[par][:, k, :], h_bank[par][:, k * 128:(k + 1) * 128],
                                               ACT.Gelu_apprx_tanh, bias=fw[par][:, 2 * F + k:2 * F + k + 1])
                ins.then_inc(h_done, 1)

            tiles(act, LEAD, SLOT_TILES, ffn_gelu)

        @block.tensor
        def _(pe):
            def gate_up(b, n):
                k, half = UNITS[n]
                if half == 0:
                    turn = b if k < 2 else 0
                    pe.wait_ge(gu_hi_done[k], turn + 1)
                    pe.wait_ge(gu_lo_done[k], turn + 1)
                wait(pe, hid_done, b * NU + n - 1)
                cols = bass.ds(b * S, S)
                for dst, base in ((g_bank[n % 2], 0), (u_bank[n % 2], F)):
                    for j in (0, 1):
                        a = base + (2 * half + j) * 128
                        o = dst[:, j * S:(j + 1) * S]
                        pe.matmul(o, gu_hi[k][:, a:a + 128], xt_hi[:, cols], start=True, stop=False)
                        pe.matmul(o, gu_hi[k][:, a:a + 128], xt_lo[:, cols], start=False, stop=False)
                        last = pe.matmul(o, gu_lo[k][:, a:a + 128], xt_hi[:, cols], start=False, stop=True)
                last.then_inc(gu_mm, 1)

            def down_proj(b, n):
                k, half = UNITS[n]
                pe.wait_ge(hid_done, b * NU + n + 1)
                if half == 0:
                    turn = b if k < 2 else 0
                    pe.wait_ge(down_in[k], 16 * (turn + 1))
                if n == 0:
                    wait(pe, s["y_read"], b)
                for j in (0, 1):
                    ch = 2 * half + j
                    last = pe.matmul(y_bank[:, 0:S], down[k][:, ch * 128:(ch + 1) * 128], hid[:, n % 3, j * S:(j + 1) * S],
                                     start=(n == 0 and j == 0), stop=(n == NU - 1 and j == 1))
                last.then_inc(slot_used[k] if half else down_mm, 1)

            pe.wait_ge(x_hi_done, 1)
            pe.wait_ge(x_lo_done, 1)

            def effective_weights():
                pe.wait_ge(const_in, 16)
                pe.wait_ge(lora_done, B)
                for j, to in ((0, x0), (1, x1)):
                    pe.matmul(to[:], const("lora_a"), lora_scaled[:, 4 * j:4 * j + 4, :], start=True, stop=True)\
                        .then_inc(eff_mm, 1)
                pe.wait_ge(eff_done, 2)
                pe.wait_ge(ones_set, 4)
                pe.wait_ge(bias_placed, 48)

            def step(n):
                if has(n, 0):
                    gate_up(n, 0)
                if has(n, 1):
                    down_proj(n - 1, NU - 2)
                if has(n, 3):
                    pe.wait_ge(s["tokt_read"], n - 2)
                    pe.wait_ge(w_now_done, n - 2)
                    pe.wait_ge(s["x1_made"], n - 2)
                    pe.matmul(x0[:, 0:S], w_now[:], x1_t[:], start=True, stop=True).then_inc(s["t_mm"], 1)
                if has(n, 0):
                    gate_up(n, 1)
                if has(n, 1):
                    down_proj(n - 1, NU - 1)
                if has(n, 3):
                    pe.wait_ge(s["t_read"], n - 2)
                    for j in (0, 1):
                        pe.transpose(x1[:, j * 2 * D:j * 2 * D + D], t_t[:, j * 128:(j + 1) * 128], const("ident"))
                        last = pe.transpose(x1[:, j * 2 * D + D:j * 2 * D + 2 * D], x1_t[:, j * 128:(j + 1) * 128], const("ident"))
                    last.then_inc(s["row_mm"], 1)
                    for j in (0, 1):
                        last = pe.matmul(x0[:, j * E:(j + 1) * E], t_t[:, j * 128:(j + 1) * 128], const("switch_w"),
                                         start=True, stop=True)
                    last.then_inc(s["logit_mm"], 1)
                if has(n, 0):
                    gate_up(n, 2)
                    if isinstance(n, int) and n == 0:
                        effective_weights()
                    down_proj(n, 0)
                if has(n, 1):
                    pe.wait_ge(s["y_read"], n)
                    wait(pe, s["v_read"], n - 1)
                    pe.matmul(x2[0:LAT, 0:S], const("wdown"), y[:], start=True, stop=True).then_inc(s["lat_mm"], 1)
                    wait(pe, s["rope_read"], 2 * (n - 1))
                    if has(n, 3):
                        pe.wait_ge(s["row_read"], n - 2)
                        pe.wait_ge(s["logit_read"], n - 2)
                    for i, (to, w) in enumerate(((x0, "wq"), (x1, "wq_swap"))):
                        pe.matmul(to[:], ones_b[0:3, :], bias_rows[:, 4 * D * i:4 * D * (i + 1)], start=True, stop=False,
                                  skip_group_check=True)
                        for j in (0, 1):
                            last = pe.matmul(to[:, j * 2 * D:j * 2 * D + D], y[:, j * 128:(j + 1) * 128], const(w),
                                             start=False, stop=False, skip_group_check=True)
                    last.then_inc(s["q_mm"], 1)
                if has(n, 0):
                    gate_up(n, 3)
                    down_proj(n, 1)
                if has(n, 1):
                    pe.wait_ge(s["lat_read"], n)
                    for to, w in ((x0, "wk"), (x1, "wk_swap")):
                        for j in (0, 1):
                            last = pe.matmul(to[:, j * 2 * D + D:j * 2 * D + 2 * D], lat[:, j * 128:(j + 1) * 128],
                                             const(w, LAT + 1), start=False, stop=True, skip_group_check=True)
                    last.then_inc(s["k_mm"], 1)
                    for j in (0, 1):
                        last = pe.matmul(x2[:, j * D:(j + 1) * D], lat[:, j * 128:(j + 1) * 128], const("wv", LAT + 1),
                                         start=True, stop=True)
                    last.then_inc(s["v_mm"], 1)
                if has(n, 0):
                    gate_up(n, 4)
                    down_proj(n, 2)
                if has(n, 2):
                    pe.wait_ge(s["rope_read"], 2 * min(n, B) if isinstance(n, int) else 2 * n)
                    if isinstance(n, int) and n > B:
                        pe.wait_ge(s["logit_read"], n - 2)
                        pe.wait_ge(s["row_read"], n - 2)
                    pe.wait_ge(s["tok_done"], n - 1)
                    for j in (0, 1):
                        last = pe.transpose(x0[:, j * 128:(j + 1) * 128], mixed_tok[:, j, :], const("ident"))
                    last.then_inc(s["tokt_mm"], 1)
                if has(n, 0):
                    gate_up(n, 5)
                    down_proj(n, 3)
                if has(n, 2):
                    pe.wait_ge(s["tokt_read"], n - 1)
                    pe.matmul(x1[:, 0:S], const("wout"), mixed_t[:], start=True, stop=True).then_inc(s["x1_mm"], 1)

            pipeline(pe, step)

            pe.wait_ge(rr, 6)
            pe.matmul(x1[:, 0:TT * E], earlier_b[:], onehot_b[:], start=True, stop=True)
            pe.matmul(x1[:, TT * E:2 * TT * E], ones_b[:], onehot_b[:], start=True, stop=True).then_inc(count_mm, 1)

            def slots_t(t, q):
                wait(pe, st_done, t - 1)
                pe.wait_ge(row_in[q], loads(t, q, RING))
                pe.transpose(st_bank[q % 2][:, 0:128], srow[q][:, 0:D], const("ident")).then_inc(st_mm, 1)

            def ffn_h(t, q):
                par = q % 2
                pe.wait_ge(w_in[par], loads(t, par, 2))
                wait(pe, h_done, t - 1)
                pe.wait_ge(st_done, t + 1)
                for k in range(FC):
                    last = pe.matmul(h_bank[par][:, k * 128:(k + 1) * 128], fw[par][:, k * 128:(k + 1) * 128], st[par],
                                     start=True, stop=True)
                last.then_inc(h_mm, 1)

            def ffn_y(t, q):
                par = q % 2
                wait(pe, y1_done, t - 1)
                pe.wait_ge(h_done, t + 1)
                for k in range(FC):
                    last = pe.matmul(fy_bank[par][:, 0:D], fh[par][:, k, :], fw[par][:, F + k * D:F + (k + 1) * D],
                                     start=(k == 0), stop=(k == FC - 1))
                last.then_inc(fy_mm, 1)

            def ffn_tile(t, q):
                ffn_h(t, q)
                if not (isinstance(t, int) and t == 0):
                    ffn_y(t - 1, (q - 1) % RING)
                if not (isinstance(t, int) and t == SLOT_TILES - 1):
                    slots_t(t + 1, (q + 1) % RING)

            pe.wait_ge(rr_slot, 1)
            slots_t(0, 0)
            tiles(pe, LEAD, SLOT_TILES - RING, ffn_tile)
            for t in range(SLOT_TILES - RING, SLOT_TILES):
                ffn_tile(t, t % RING)
            ffn_y(SLOT_TILES - 1, (SLOT_TILES - 1) % RING)

        @block.vector
        def _(dve):
            done = [0]

            def chain(ins):
                done[0] += 1
                ins.then_inc(rt, 1)
                dve.wait_ge(rt, done[0])

            dve.wait_ge(cond_in, 16)
            chain(nc.vector.reduce_max(r_max[:], cb[:], AX))
            chain(nc.vector.tensor_tensor(r_exp[:], cb[:], r_max[:].unsqueeze(2).broadcast_to([128, B, E]), ALU.subtract))
            dve.wait_ge(r_expd, 1)
            chain(nc.vector.reduce_sum(r_sum[:], r_exp[:], AX))
            chain(nc.vector.reciprocal(r_sum[:], r_sum[:]))
            chain(nc.vector.tensor_tensor(r_prob[:], r_exp[:], r_sum[:].unsqueeze(2).broadcast_to([128, B, E]), ALU.mult))
            for b in range(B):
                ins = nc.vector.max(r_top[:, b, :], r_prob[:, b, :])
            chain(ins)
            for b in range(B):
                ins = nc.vector.max_index(chosen[:, b, :], r_top[:, b, :], r_prob[:, b, :])
            ins.then_inc(chosen_done, 1)
            chain(nc.vector.reduce_sum(r_norm[:], r_top[:, :, 0:TOP_K], AX))
            chain(nc.vector.reciprocal(r_norm[:], r_norm[:]))
            chain(nc.vector.tensor_tensor(r_w[:], r_top[:, :, 0:TOP_K], r_norm[:].unsqueeze(2).broadcast_to([128, B, TOP_K]),
                                          ALU.mult))
            chain(nc.vector.tensor_scalar(r_part[:], r_w[:], 1.0 - 1.0 / MOE_LAYERS, None, ALU.mult))
            chain(nc.vector.scalar_tensor_tensor(weight[:, :, 0:TOP_K], r_w[:], 1.0 / MOE_LAYERS, r_part[:], ALU.mult, ALU.add))
            nc.vector.memset(weight[:, :, TOP_K:TOP_K + 1], 1.0).then_inc(weight_done, 1)
            dve.wait_ge(weight_done, 1)

            dve.wait_ge(x_in, 16)
            nc.vector.tensor_copy(xt_hi[:], xt[:]).then_inc(x_hi_done, 1)
            dve.wait_ge(x_hi_done, 1)
            nc.vector.tensor_tensor(xt_lo[:], xt[:], xt_hi[:].bitcast(F32), ALU.subtract).then_inc(x_lo_done, 1)
            weights = weight[:].rearrange("p b k -> p (b k)")

            def unit(b, n):
                k, half = UNITS[n]
                dve.wait_ge(gelu_done, b * NU + n + 1)
                if half == 0:
                    pk, turn = UNITS[(n - 3) % NU][0], (b if n >= 3 else b - 1)
                    wait(dve, slot_used[pk], turn + 1)
                else:
                    wait(dve, down_mm, b * (NU // 2) + (n - 3) // 2 + 1)
                nc.vector.scalar_tensor_tensor(hid[:, n % 3, :], u_bank[n % 2], weights[:, bass.ds(b * (TOP_K + 1) + k, 1)],
                                               gelu[:, n % 2, :], ALU.mult, ALU.mult).then_inc(hid_done, 1)


            def effective_weights():
                dve.wait_ge(const_in, 16)
                for b in range(B):
                    cond_b = const("cond_rows")[:, b:b + 1]
                    nc.vector.tensor_scalar(lora_scaled[:, b, :], const("lora_b"), cond_b, 2.0, ALU.mult, ALU.mult)\
                        .then_inc(lora_done, 1)
                dve.wait_ge(bias_in, 16)
                nc.vector.tensor_copy(bias_split[:, 0, :], bias_in_f[:]).then_inc(bias_done, 1)
                dve.wait_ge(bias_done, 1)
                chain(nc.vector.tensor_tensor(bias_rest[:], bias_in_f[:], bias_split[:, 0, :], ALU.subtract))
                nc.vector.tensor_copy(bias_split[:, 1, :], bias_rest[:]).then_inc(bias_done, 1)
                dve.wait_ge(bias_done, 2)
                nc.vector.tensor_tensor(bias_split[:, 2, :], bias_rest[:], bias_split[:, 1, :], ALU.subtract)\
                    .then_inc(bias_done, 1)
                for j, of in ((0, x0), (1, x1)):
                    dve.wait_ge(eff_mm, j + 1)
                    nc.vector.tensor_tensor(w_eff[:, 4 * j:4 * j + 4, :], of[:].rearrange("p (b o) -> p b o", b=4),
                                            const("wbase").unsqueeze(1).broadcast_to([128, 4, D]), ALU.add).then_inc(eff_done, 1)
                dve.wait_ge(eff_done, 2)

            def step(n):
                if has(n, 3):
                    pe_passed = n - 1 if not isinstance(n, int) else min(n - 1, B)
                    dve.wait_ge(s["q_mm"], pe_passed)
                    nc.vector.tensor_copy(w_now[:], w_eff[:].rearrange("p b o -> p (b o)")[:, bass.ds((n - 3) * D, D)])\
                        .then_inc(w_now_done, 1)
                    if isinstance(n, int) and n > B:
                        dve.wait_ge(s["row_mm"], n - 3)
                    dve.wait_ge(s["x1_mm"], n - 2)
                    nc.vector.scalar_tensor_tensor(x1_t[:], x1[:, 0:S], const("bout"), xt[:, bass.ds((n - 3) * S, S)],
                                                   ALU.add, ALU.add).then_inc(s["x1_made"], 1)
                if has(n, 0):
                    unit(n, 0)
                    unit(n, 1)
                    if isinstance(n, int) and n == 0:
                        effective_weights()
                if has(n, 3):
                    dve.wait_ge(s["logit_mm"], n - 2)
                    dst = logit[:].rearrange("p t e -> p (t e)")[:, bass.ds((n - 3) * 2 * E, 2 * E)]
                    nc.vector.tensor_tensor(dst.rearrange("p (t e) -> p t e", e=E),
                                            x0[:, 0:2 * E].rearrange("p (t e) -> p t e", e=E),
                                            const("switch_b").unsqueeze(1).broadcast_to([128, 2, E]), ALU.add)\
                        .then_inc(s["logit_read"], 1)
                if has(n, 2):
                    dve.wait_ge(s["exp_done"], n - 1)
                    nc.vector.reduce_sum(den[:], prob[:], AX).then_inc(s["sum_done"], 1)
                    values_sum(n, 0)
                if has(n, 0):
                    unit(n, 2)
                if has(n, 2):
                    dve.wait_ge(s["sum_done"], n - 1)
                    nc.vector.reciprocal(den[:], den[:]).then_inc(s["recip_done"], 1)
                    values_sum(n, 1)
                    dve.wait_ge(s["recip_done"], n - 1)
                    dve.wait_ge(s["pv_done"], 2 * (n - 1))
                    wait(dve, s["tokt_mm"], n - 2)
                    nc.vector.tensor_tensor(mixed_tok[:].rearrange("p t (h d) -> p t h d", d=DH), mixed[:],
                                            den[:].unsqueeze(3).broadcast_to([128, 2, NH, DH]), ALU.mult)\
                        .then_inc(s["tok_done"], 1)
                if has(n, 0):
                    unit(n, 3)
                if has(n, 1):
                    dve.wait_ge(s["k_mm"], n)
                    for i, (of, table) in enumerate(((x0, "cos"), (x1, "sin"))):
                        nc.vector.tensor_tensor(rope[:, i, :], of[:], const(table), ALU.mult).then_inc(s["rope_read"], 1)
                    dve.wait_ge(s["rope_read"], 2 * n)
                    nc.vector.tensor_tensor(qk[:].rearrange("p t j h d -> p (t j h d)"), rope[:, 0, :], rope[:, 1, :],
                                            ALU.add).then_inc(s["turned"], 1)
                    dve.wait_ge(s["turned"], n)
                    qk_product(n, 0)
                if has(n, 0):
                    unit(n, 4)
                if has(n, 1):
                    qk_product(n, 1)
                    qk_sum(n, 0)
                if has(n, 0):
                    unit(n, 5)
                if has(n, 1):
                    qk_sum(n, 1)
                    dve.wait_ge(s["score_done"], 2 * n)
                    nc.vector.reduce_max(s_max[:], score[:], AX).then_inc(s["max_done"], 1)
                    dve.wait_ge(s["max_done"], n)
                    nc.vector.tensor_tensor(score[:], score[:], s_max[:].unsqueeze(3).broadcast_to([128, 2, NH, NH]),
                                            ALU.subtract).then_inc(s["sub_done"], 1)

            def values_sum(n, tile):
                dve.wait_ge(s["pv_prod_done"], 2 * (n - 2) + tile + 1)
                nc.vector.reduce_sum(mixed[:, tile], pv_prod[:, tile], AX).then_inc(s["pv_done"], 1)

            def qk_product(n, tile):
                nc.vector.tensor_tensor(qk_prod[:, tile], qk[:, tile, 0].unsqueeze(2).broadcast_to([128, NH, NH, DH]),
                                        qk[:, tile, 1].unsqueeze(1).broadcast_to([128, NH, NH, DH]), ALU.mult)\
                    .then_inc(s["qk_prod_done"], 1)

            def qk_sum(n, tile):
                dve.wait_ge(s["qk_prod_done"], 2 * (n - 1) + tile + 1)
                if tile == 0:
                    wait(dve, s["exp_done"], n - 1)
                nc.vector.reduce_sum(score[:, tile], qk_prod[:, tile], AX).then_inc(s["score_done"], 1)

            pipeline(dve, step)

            steps = [0]

            def link(ins):
                steps[0] += 1
                ins.then_inc(rr, 1)
                dve.wait_ge(rr, steps[0])

            def over_experts(ap):
                return ap.unsqueeze(2).broadcast_to([128, TT, E])

            dve.wait_ge(s["logit_read"], B)
            link(nc.vector.reduce_max(l_max[:], logit[:], AX))
            link(nc.vector.tensor_tensor(l_exp[:], logit[:], over_experts(l_max[:]), ALU.subtract))
            dve.wait_ge(rr_exp, 1)
            link(nc.vector.scalar_tensor_tensor(l_eq[:], l_exp[:], 1.0, const("falling").unsqueeze(1).broadcast_to([128, TT, E]),
                                                ALU.is_ge, ALU.mult))
            link(nc.vector.reduce_max(l_first[:], l_eq[:], AX))
            link(nc.vector.tensor_tensor(onehot[:], l_eq[:], over_experts(l_first[:]), ALU.is_equal))
            nc.vector.tensor_copy(earlier_b[:], const("earlier_row"))
            link(nc.vector.tensor_copy(onehot_b[:], onehot[:].rearrange("p t e -> p (t e)")))
            link(nc.vector.reduce_sum(l_sum[:], l_exp[:], AX))
            dve.wait_ge(s["row_read"], B)
            dve.wait_ge(ids_in, 16)
            nc.vector.reciprocal(rows[:, :, PROB], l_sum[:]).then_inc(rr_cols, 1)
            nc.vector.tensor_copy(rows[:, :, IDX].bitcast(I32), ids[:]).then_inc(rr_cols, 1)
            dve.wait_ge(count_mm, 1)
            link(nc.vector.tensor_copy(total[:], x1[:, TT * E:2 * TT * E].rearrange("p (t e) -> p t e", e=E)))
            src, k, shift = total, 0, 1
            while shift < TT:
                dst = scan[k % 2]
                nc.vector.tensor_copy(dst[:, 0:shift, :], src[:, 0:shift, :])
                link(nc.vector.tensor_tensor(dst[:, shift:, :], src[:, shift:, :], src[:, 0:TT - shift, :], ALU.add))
                src, k, shift = dst, k + 1, 2 * shift
            link(nc.vector.tensor_tensor(over[:], src[:, TT - 1, :].unsqueeze(2).broadcast_to([128, E, TT]),
                                         const("ramp").unsqueeze(1).broadcast_to([128, E, TT]), ALU.is_gt))
            link(nc.vector.reduce_sum(n_tiles[:], over[:], AX))
            link(nc.vector.tensor_tensor(prev_tiles[:], n_tiles[:].unsqueeze(1).broadcast_to([128, E, E]),
                                         const("before").rearrange("p (a b) -> p a b", a=E), ALU.mult))
            link(nc.vector.reduce_sum(first_tile[:], prev_tiles[:], AX))
            link(nc.vector.tensor_tensor(end_tile[:], first_tile[:], n_tiles[:], ALU.add))
            link(nc.vector.tensor_tensor(place[:], src[:], total[:], ALU.subtract))
            link(nc.vector.tensor_tensor(place[:], x1[:, 0:TT * E].rearrange("p (t e) -> p t e", e=E), place[:], ALU.add))
            link(nc.vector.scalar_tensor_tensor(place[:], first_tile[:].unsqueeze(1).broadcast_to([128, TT, E]), 128.0, place[:],
                                                ALU.mult, ALU.add))
            link(nc.vector.tensor_tensor(place[:], place[:], onehot[:], ALU.mult))
            link(nc.vector.reduce_sum(slot_f[:], place[:], AX))
            nc.vector.tensor_copy(slot[:], slot_f[:]).then_inc(rr_slot, 1)
            link(nc.vector.tensor_tensor(ended[:], end_tile[:].unsqueeze(1).broadcast_to([128, SLOT_TILES, E]),
                                         const("slot_tile").unsqueeze(2).broadcast_to([128, SLOT_TILES, E]), ALU.is_le))
            link(nc.vector.reduce_sum(owner_f[:], ended[:], AX))
            nc.vector.tensor_scalar(owner[:], owner_f[:], float(E - 1), None, ALU.min).then_inc(rr_owner, 1)

            def ffn_st(t, q):
                wait(dve, h_mm, t - 1)
                dve.wait_ge(st_mm, t + 1)
                nc.vector.tensor_copy(st[q % 2], st_bank[q % 2][:, 0:128]).then_inc(st_done, 1)

            def ffn_out(t, q):
                par = q % 2
                wait(dve, z_done, t)
                dve.wait_ge(fy_mm, t + 1)
                nc.vector.tensor_tensor(y1[:], fy_bank[par][:, 0:D], fw[par][:, 2 * F + FC:], ALU.add).then_inc(y1_done, 1)
                wait(dve, yo_done, t - 1)
                dve.wait_ge(y1_done, t + 1)
                nc.vector.tensor_scalar(z[par], y1[:], srow[q][:, PROB:PROB + 1], None, ALU.mult).then_inc(z_done, 1)

            def ffn_tile(t, q):
                ffn_out(t, q)
                if not (isinstance(t, int) and t >= SLOT_TILES - 2):
                    ffn_st(t + 2, (q + 2) % RING)

            ffn_st(0, 0)
            ffn_st(1, 1)
            tiles(dve, LEAD, SLOT_TILES - RING, ffn_tile)
            for t in range(SLOT_TILES - RING, SLOT_TILES):
                ffn_tile(t, t % RING)


def kernel(**inputs):
    import numpy as np
    import concourse.bacc as bacc
    from concourse.bass_utils import run_bass_kernel_spmd

    a = {k: np.asarray(val) for k, val in inputs.items()}
    x_t = np.ascontiguousarray(a["x"].reshape(T, D).T)

    def chunked(w):
        return w.reshape(*w.shape[:-2], FC, 128, D).swapaxes(-3, -2).reshape(*w.shape[:-2], 128, FC * D)

    skill = np.concatenate([a["L0_cond_skill_gate"], a["L0_cond_skill_up"], chunked(a["L0_cond_skill_down"])], axis=2)
    shared = np.concatenate([a["L0_cond_shared_gate"], a["L0_cond_shared_up"], chunked(a["L0_cond_shared_down"])], axis=1)
    experts = np.ascontiguousarray(np.concatenate([skill, shared[None]], axis=0))
    ffn = np.ascontiguousarray(np.concatenate([
        a["L0_ffn_w1"], chunked(a["L0_ffn_w2"]), a["L0_ffn_b1"].reshape(E, FC, 128).swapaxes(1, 2),
        np.broadcast_to(a["L0_ffn_b2"][:, None, :], (E, 128, D))], axis=2))
    cond = np.ascontiguousarray(np.broadcast_to(a["cond_8"].reshape(1, B * E), (128, B * E)))

    pos = np.arange(S, dtype=np.float32)
    freq = (1.0 / np.float32(10000.0) ** (np.arange(0, DH, 2, dtype=np.float32) / DH)).astype(np.float32)
    angle = (pos[:, None] * freq[None, :]).astype(np.float32)
    half = DH // 2
    feature = np.arange(D)
    sign = np.where(feature % DH < half, -1, 1).astype(np.float32)
    cos = np.tile(np.cos(angle).astype(np.float32)[:, feature % half].reshape(2, 128, 1, D), (1, 1, 2, 1))
    sin = np.tile((np.sin(angle).astype(np.float32)[:, feature % half] * sign).reshape(2, 128, 1, D), (1, 1, 2, 1))
    cos, sin = (a_.transpose(1, 0, 2, 3).reshape(128, 4 * D) for a_ in (cos, sin))
    swap = (feature // DH) * DH + (feature % DH + half) % DH
    k_cols = (feature // DH) * 2 * DH + feature % DH
    up = np.concatenate([a["L0_attn_Wup"], a["L0_attn_bup"][None]], axis=0)
    order = np.arange(128)
    r = a["L0_cond2_As"].shape[1]
    full = {
        "switch_b": np.broadcast_to(a["L0_ffn_switch_b"][None], (128, E)),
        "cond_rows": np.repeat(a["cond_8"].T, r, axis=0),
        "wq": a["L0_attn_Wq"], "wq_swap": a["L0_attn_Wq"][:, swap],
        "wk": up[:, k_cols], "wk_swap": up[:, k_cols[swap]], "wv": up[:, k_cols + DH],
        "wdown": a["L0_attn_Wdown"],
        "bdown": a["L0_attn_bdown"][:, None], "wout": a["L0_attn_Wout"], "bout": a["L0_attn_bout"][:, None],
        "wbase": a["L0_cond2_W_base"].T, "bbase": a["L0_cond2_b_base"][:, None],
        "lora_a": a["L0_cond2_As"].reshape(E * r, D), "lora_b": a["L0_cond2_Bs"].swapaxes(1, 2).reshape(E * r, D),
        "switch_w": a["L0_ffn_switch_w"], "cos": cos, "sin": sin, "ident": np.eye(128, dtype=np.float32),
        "earlier_row": (order[:, None] < order[None, :]).astype(np.float32),
        "falling": np.broadcast_to(np.arange(E, 0, -1, dtype=np.float32), (128, E)),
        "ramp": np.broadcast_to(128 * np.arange(TT, dtype=np.float32), (128, TT)),
        "before": np.broadcast_to((np.arange(E)[None, :] < np.arange(E)[:, None]).astype(np.float32).reshape(1, E * E),
                                  (128, E * E)),
        "slot_tile": np.broadcast_to(np.arange(SLOT_TILES, dtype=np.float32), (128, SLOT_TILES)),
    }
    consts = np.zeros((128, CONST_W), np.float32)
    for name, (at, width) in AT.items():
        consts[:full[name].shape[0], at:at + width] = full[name]
    query_bias = np.zeros((2, 2, 2, D), np.float32)
    query_bias[0, :, 0], query_bias[1, :, 0] = a["L0_attn_bq"], a["L0_attn_bq"][swap]
    query_bias = query_bias.reshape(1, 8 * D)
    token_ids = np.ascontiguousarray(np.arange(T, dtype=np.int32).reshape(TT, 128).T)

    arrays = {"in_x_t": x_t, "in_cond": cond, "in_experts": experts, "in_ffn": ffn, "in_consts": consts, "in_query_bias": query_bias,
              "in_token_ids": token_ids}
    nc = bacc.Bacc("TRN2", target_bir_lowering=False, num_devices=1)
    args = [nc.dram_tensor(name, v.shape, mybir.dt.from_np(v.dtype), kind="ExternalInput").ap() for name, v in arrays.items()]
    out = nc.dram_tensor("out", (T, D), F32, kind="ExternalOutput").ap()
    adaln_program(nc, *args, out)
    r = run_bass_kernel_spmd(nc, [arrays], core_ids=[0])
    return r.results[0]["out"].reshape(B, S, D)
```

```python
from contextlib import ExitStack

import concourse.bass as bass
from concourse import mybir

F32 = mybir.dt.float32
F32R = mybir.dt.float32r
BF16 = mybir.dt.bfloat16
U32 = mybir.dt.uint32
I32 = mybir.dt.int32
ACT = mybir.ActivationFunctionType
ALU = mybir.AluOpType
AX = mybir.AxisListType.X

B, S, D = 8, 256, 128
T = B * S
E, F = 8, 512
NH, DH = 16, 8
LAT = 32
TOP_K, MOE_LAYERS = 2, 12
FC = F // 128
TT = T // 128
SLOT_TILES = TT + E - 1
SLOTS = SLOT_TILES * 128
PROB, IDX, ROW = 2 * D, 2 * D + 1, 2 * D + 2
NO_TOKEN = 1 << 20
RING = 8
LEAD = SLOT_TILES % RING
HOT_W = F + FC + D
FFN_W = HOT_W + F

FIELDS = [("switch_b", E), ("cond_rows", B), ("wq", D), ("wq_swap", D), ("wk", D), ("wk_swap", D), ("wv", D),
          ("wdown", LAT), ("bdown", 1), ("wout", D), ("bout", 1), ("wbase", D),
          ("bbase", 1), ("lora_a", D), ("lora_b", D), ("switch_w", E), ("cos", 4 * D), ("sin", 4 * D), ("ident", D),
          ("earlier_row", D), ("falling", E), ("ramp", TT), ("before", E * E), ("slot_tile", SLOT_TILES)]
AT, CONST_W = {}, 0
for _name, _width in FIELDS:
    AT[_name] = (CONST_W, _width)
    CONST_W += _width


def adaln_program(nc, x_t, cond, experts, ffn, consts, query_bias, token_ids, out):
    ctx = ExitStack()
    with ctx:
        first = ctx.enter_context(ExitStack())

        def sb(name, shape, dt=F32, at=ctx):
            return at.enter_context(nc.sbuf_tensor(name, shape, dt))

        def sem(name):
            return ctx.enter_context(nc.semaphore(name))

        gu_bank = [ctx.enter_context(nc.psum_tensor(f"gu_bank{i}", [128, 2, 512], F32)) for i in (0, 1)]
        y_bank, x0, x1, x2 = [ctx.enter_context(nc.psum_tensor(n, [128, 512], F32)) for n in ("y_bank", "x0", "x1", "x2")]

        slot_dram = nc.dram_tensor("slot_dram", [SLOTS, ROW], F32).ap()

        gu, gu_hi, gu_lo, down = ([sb(f"{n}{k}", [128, w], dt, at=first) for k in range(3)] for n, w, dt in (
            ("gu", 2 * F, F32), ("gu_hi", 2 * F, F32R), ("gu_lo", 2 * F, F32R), ("down", F, F32)))
        first.close()
        fw = sb("fw", [128, 3 * 7 * F])[:, 0:E * FFN_W].rearrange("p (e w) -> p e w", e=E)

        c = sb("c", [128, CONST_W])
        cb = sb("cb", [128, B, E])
        ids = sb("ids", [128, TT], I32)
        xt = sb("xt", [128, T])

        def const(name, rows=128):
            a, w = AT[name]
            return c[0:rows, a:a + w]

        r_max = sb("r_max", [128, B])
        r_exp = sb("r_exp", [128, B, E])
        r_sum = sb("r_sum", [128, B])
        r_prob = sb("r_prob", [128, B, E])
        r_top = sb("r_top", [128, B, 8])
        chosen = sb("chosen", [128, B, 8], U32)
        r_norm = sb("r_norm", [128, B])
        r_w = sb("r_w", [128, B, TOP_K])
        r_part = sb("r_part", [128, B, TOP_K])
        weight = sb("weight", [128, B, TOP_K + 1])

        xt_hi = sb("xt_hi", [128, T], F32R)
        xt_lo = sb("xt_lo", [128, T], F32R)
        gelu = sb("gelu", [128, 2, 512])
        hid = sb("hid", [128, 3, 512])

        lora_scaled = sb("lora_scaled", [128, B, D])
        w_eff = sb("w_eff", [128, B, D])
        w_now = sb("w_now", [128, D])
        bias_in_f = sb("bias_in_f", [1, 8 * D])
        bias_rest = sb("bias_rest", [1, 8 * D])
        bias_split = sb("bias_split", [1, 3, 8 * D], BF16)
        bias_rows = sb("bias_rows", [3, 8 * D], BF16)
        y = sb("y", [128, S])
        lat = sb("lat", [LAT + 1, S])
        rope = sb("rope", [128, 2, 4 * D])
        qk = sb("qk", [128, 2, 2, NH, DH])
        qk_prod = sb("qk_prod", [128, 2, NH, NH, DH])
        score = sb("score", [128, 2, NH, NH])
        s_max = sb("s_max", [128, 2, NH])
        prob = sb("prob", [128, 2, NH, NH])
        v = sb("v", [128, 2, DH, NH])
        pv_prod = sb("pv_prod", [128, 2, NH, DH, NH])
        mixed = sb("mixed", [128, 2, NH, DH])
        den = sb("den", [128, 2, NH])
        mixed_tok = sb("mixed_tok", [128, 2, D])
        mixed_t = sb("mixed_t", [128, S])
        x1_t = sb("x1_t", [128, S])
        t_t = sb("t_t", [128, S])
        rows = sb("rows", [128, TT, ROW])
        logit = sb("logit", [128, TT, E])

        l_max = sb("l_max", [128, TT])
        l_exp = sb("l_exp", [128, TT, E])
        l_sum = sb("l_sum", [128, TT])
        l_eq = sb("l_eq", [128, TT, E])
        l_first = sb("l_first", [128, TT])
        onehot = sb("onehot", [128, TT, E])
        onehot_b = sb("onehot_b", [128, TT * E], BF16)
        earlier_b = sb("earlier_b", [128, 128], BF16)
        ones_b = sb("ones_b", [128, 128], BF16)
        total = sb("total", [128, TT, E])
        scan = [sb(f"scan{i}", [128, TT, E]) for i in (0, 1)]
        over = sb("over", [128, E, TT])
        n_tiles = sb("n_tiles", [128, E])
        prev_tiles = sb("prev_tiles", [128, E, E])
        first_tile = sb("first_tile", [128, E])
        end_tile = sb("end_tile", [128, E])
        place = sb("place", [128, TT, E])
        slot_f = sb("slot_f", [128, TT])
        slot = sb("slot", [128, TT], U32)
        ended = sb("ended", [128, SLOT_TILES, E])
        owner_f = sb("owner_f", [128, SLOT_TILES])
        owner = sb("owner", [128, SLOT_TILES], U32)
        empty = sb("empty", [128, ROW])

        srow = [pv_prod[:].rearrange("p a b c d -> p (a b c d)")[:, i * ROW:(i + 1) * ROW] for i in range(RING)]
        hot = [qk_prod[:].rearrange("p a b c d -> p (a b c d)")[:, i * HOT_W:(i + 1) * HOT_W] for i in range(4)]
        st = [hid[:, 2, i * 128:(i + 1) * 128] for i in (0, 1)]
        fh = [gelu[:, i, :].rearrange("p (k s) -> p k s", k=FC) for i in (0, 1)]
        y1 = [hid[:, i, 0:D] for i in (0, 1)]
        z = [hid[:, i, D:2 * D] for i in (0, 1)]

        cond_in, const_in, ids_in = sem("cond_in"), sem("const_in"), sem("ids_in")
        x_in = [sem("x_in_first"), sem("x_in_rest")]
        gu_in = [sem(f"gu_in{k}") for k in range(3)]
        down_in = [sem(f"down_in{k}") for k in range(3)]
        empty_out = sem("empty_out")
        rt, r_expd, chosen_done, weight_done = sem("rt"), sem("r_expd"), sem("chosen_done"), sem("weight_done")
        x_hi_done, x_lo_done = sem("x_hi_done"), sem("x_lo_done")
        gu_hi_done = [sem(f"gu_hi_done{k}") for k in range(3)]
        gu_lo_done = [sem(f"gu_lo_done{k}") for k in range(3)]
        slot_used = [sem(f"slot_used{k}") for k in range(3)]
        gu_mm, gelu_done, hid_done, down_mm = (
            sem(n) for n in ("gu_mm", "gelu_done", "hid_done", "down_mm"))
        lora_done, eff_mm, eff_done, w_now_done = sem("lora_done"), sem("eff_mm"), sem("eff_done"), sem("w_now_done")
        ones_set, bias_in, bias_done, bias_placed = sem("ones_set"), sem("bias_in"), sem("bias_done"), sem("bias_placed")
        names = ("y_read lat_mm lat_read q_mm k_mm v_mm v_read rope_read turned qk_prod_done0 qk_prod_done1 score_done max_done sub_done "
                 "exp_done pv_prod_done pv_done sum_done recip_done tok_done tokt_mm tokt_read x1_mm x1_made t_mm t_read "
                 "row_mm row_read logit_mm logit_read")
        s = {n: sem(n) for n in names.split()}
        (rr, rr_exp, count_mm, rr_slot, rr_owner, rr_cols, scattered, ffn_in, hot_done, st_mm, st_done, h_mm, h_done, fy_mm,
         y1_done, z_done, yo_done) = (
            sem(n) for n in ("rr", "rr_exp", "count_mm", "rr_slot", "rr_owner", "rr_cols", "scattered", "ffn_in",
                             "hot_done", "st_mm", "st_done", "h_mm", "h_done", "fy_mm", "y1_done", "z_done", "yo_done"))
        row_in, stored = ([sem(f"{n}{i}") for i in range(RING)] for n in ("row_in", "stored"))

        def wait(eng, semaphore, value):
            if not (isinstance(value, int) and value <= 0):
                eng.wait_ge(semaphore, value)

        def at(i, o):
            return RING * i + o

        def fills(i, o):
            return 16 * (i + o // RING) + 16

        def tiles(eng, lead, end, body):
            for t in range(lead):
                body(0, t)
            with eng.Fori(0, (end - lead) // RING) as i:
                for j in range(RING):
                    body(i, lead + j)

        def pipeline(eng, step):
            for n in range(3):
                step(n)
            with eng.Fori(3, B) as n:
                step(n)
            for n in range(B, B + 3):
                step(n)

        def has(n, lag):
            return not isinstance(n, int) or 0 <= n - lag < B

        UNITS = [(k, half) for k in (2, 0, 1) for half in (0, 1)]
        NU = len(UNITS)

        def used_by(b, k):
            return (b - 1) * NU + UNITS.index((k, 1)) + 1 if not (isinstance(b, int) and b == 0) else 0

        g_bank = [gu_bank[i][:, 0, :] for i in (0, 1)]
        u_bank = [gu_bank[i][:, 1, :] for i in (0, 1)]
        h_bank, st_bank, fy_bank = g_bank, [x0, x1], [x2, y_bank]

        block = ctx.enter_context(nc.Block())

        @block.sync
        def _(sp):
            sp.dma_start(cb[:].rearrange("p b e -> p (b e)"), cond).then_inc(cond_in, 16)
            sp.dma_start(gu[2][:], experts[E, :, 0:2 * F]).then_inc(gu_in[2], 16)
            sp.dma_start(xt[:, 0:S], x_t[:, 0:S]).then_inc(x_in[0], 16)
            sp.dma_start(down[2][:], experts[E, :, 2 * F:3 * F]).then_inc(down_in[2], 16)
            sp.wait_ge(chosen_done, 1)

            def expert_load(b, k):
                e = sp.value_load(chosen[0:1, b, k:k + 1] if isinstance(b, int) else
                                  chosen[:].rearrange("p b e -> p (b e)")[0:1, bass.ds(b * 8 + k, 1)],
                                  min_val=0, max_val=E - 1)
                src = experts[bass.ds(e, 1)].rearrange("a p f -> p (a f)")
                wait(sp, gu_hi_done[k], b)
                wait(sp, gu_lo_done[k], b)
                sp.dma_start(gu[k][:], src[:, 0:2 * F]).then_inc(gu_in[k], 16)
                wait(sp, slot_used[k], b)
                sp.dma_start(down[k][:], src[:, 2 * F:3 * F]).then_inc(down_in[k], 16)

            expert_load(0, 0)
            expert_load(0, 1)
            sp.dma_start(xt[:, S:], x_t[:, S:]).then_inc(x_in[1], 16)
            sp.dma_start(c[:], consts).then_inc(const_in, 16)
            sp.dma_start(bias_in_f[:], query_bias).then_inc(bias_in, 16)
            sp.dma_start(ids[:], token_ids).then_inc(ids_in, 16)
            expert_load(1, 0)
            expert_load(1, 1)
            sp.wait_ge(bias_done, 3)
            for i in range(3):
                sp.dma_start(bias_rows[i:i + 1, :], bias_split[:, i, :]).then_inc(bias_placed, 16)
            sp.wait_ge(ones_set, 4)
            for i in range(SLOT_TILES):
                sp.dma_start(slot_dram[i * 128:(i + 1) * 128, :], empty[:]).then_inc(empty_out, 16)
            with sp.Fori(2, B) as b:
                expert_load(b, 0)
                expert_load(b, 1)

            sp.wait_ge(slot_used[1], B)
            for e in range(E):
                sp.dma_start(fw[:, e, :], ffn[e]).then_inc(ffn_in, 16)
            sp.wait_ge(scattered, 16 * TT)

            for t in range(SLOT_TILES):
                wait(sp, stored[t % RING], fills(0, t - RING))
                sp.dma_start(srow[t % RING], slot_dram[t * 128:(t + 1) * 128, :]).then_inc(row_in[t % RING], 16)
            for t in range(SLOT_TILES - RING, SLOT_TILES):
                sp.wait_ge(stored[t % RING], fills(0, t))

        @block.gpsimd
        def _(pool):
            nc.gpsimd.memset(ones_b[:], 1.0).then_inc(ones_set, 1)
            nc.gpsimd.memset(lat[:], 1.0).then_inc(ones_set, 1)
            nc.gpsimd.memset(empty[:], 0.0).then_inc(ones_set, 1)
            pool.wait_ge(ones_set, 3)
            nc.gpsimd.memset(empty[:, IDX:IDX + 1].bitcast(I32), NO_TOKEN).then_inc(ones_set, 1)
            pool.wait_ge(ones_set, 4)
            def low(b, k):
                pool.wait_ge(gu_in[k], 16 * b + 16)
                pool.wait_ge(gu_hi_done[k], b + 1)
                wait(pool, gu_mm, used_by(b, k))
                nc.gpsimd.tensor_tensor(gu_lo[k][:], gu[k][:], gu_hi[k][:].bitcast(F32), ALU.subtract)\
                    .then_inc(gu_lo_done[k], 1)

            low(0, 2)

            def step(n):
                for tile in (0, 1):
                    if has(n, 0):
                        low(n, tile)
                    if has(n, 2):
                        pool.wait_ge(s["v_read"], n - 1)
                        wait(pool, s["pv_done"], 2 * (n - 2) + tile - 1 if tile else 2 * (n - 2))
                        pool.wait_ge(s["exp_done"], n - 1)
                        nc.gpsimd.tensor_tensor(pv_prod[:, tile], prob[:, tile].unsqueeze(2).broadcast_to([128, NH, DH, NH]),
                                                v[:, tile].unsqueeze(1).broadcast_to([128, NH, DH, NH]), ALU.mult)\
                            .then_inc(s["pv_prod_done"], 1)
                if has(n, 1):
                    wait(pool, s["score_done"], 2 * (n - 1))
                    pool.wait_ge(s["turned"], n)
                    nc.gpsimd.tensor_tensor(qk_prod[:, 1], qk[:, 1, 0].unsqueeze(2).broadcast_to([128, NH, NH, DH]),
                                            qk[:, 1, 1].unsqueeze(1).broadcast_to([128, NH, NH, DH]), ALU.mult)\
                        .then_inc(s["qk_prod_done1"], 1)

            pipeline(pool, step)

            pool.wait_ge(empty_out, 16 * SLOT_TILES)
            pool.wait_ge(s["row_read"], B)
            pool.wait_ge(rr_cols, 2)
            pool.wait_ge(rr_slot, 1)
            for i in range(TT):
                pool.indirect_dma_start(slot_dram, bass.IndirectOffsetOnAxis(slot[:, i:i + 1], 0),
                                        rows[:, i, :], None).then_inc(scattered, 16)

            def store(q):
                pool.indirect_dma_start(out, bass.IndirectOffsetOnAxis(srow[q][:, IDX:IDX + 1].bitcast(U32), 0),
                                        srow[q][:, D:2 * D], None, bounds_check=T - 1, oob_is_err=False)\
                    .then_inc(stored[q], 16)

            def add_x1(i, o):
                t, q = at(i, o), o % RING
                wait(pool, yo_done, t)
                pool.wait_ge(z_done, t + 1)
                nc.gpsimd.tensor_tensor(srow[q][:, D:2 * D], z[q % 2], srow[q][:, D:2 * D], ALU.add).then_inc(yo_done, 1)
                if not (isinstance(t, int) and t == 0):
                    store((q - 1) % RING)

            tiles(pool, LEAD, SLOT_TILES, add_x1)
            pool.wait_ge(yo_done, SLOT_TILES)
            store((SLOT_TILES - 1) % RING)
            for t in range(SLOT_TILES - RING, SLOT_TILES):
                pool.wait_ge(stored[t % RING], fills(0, t))

        @block.scalar
        def _(act):
            act.wait_ge(rt, 2)
            nc.scalar.activation(r_exp[:], r_exp[:], ACT.Exp).then_inc(r_expd, 1)

            def high(b, k):
                act.wait_ge(gu_in[k], 16 * b + 16)
                wait(act, gu_mm, used_by(b, k))
                nc.scalar.activation(gu_hi[k][:], gu[k][:], ACT.Copy).then_inc(gu_hi_done[k], 1)

            def unit(b, n):
                act.wait_ge(gu_mm, b * NU + n + 1)
                wait(act, hid_done, b * NU + n - 1)
                nc.scalar.activation(gelu[:, n % 2, :], g_bank[n % 2], ACT.Gelu_apprx_tanh).then_inc(gelu_done, 1)

            high(0, 2)

            def step(n):
                if isinstance(n, int) and n == 1:
                    act.wait_ge(const_in, 16)
                    act.wait_ge(ones_set, 4)
                if has(n, 0):
                    high(n, 0)
                if has(n, 0):
                    unit(n, 0)
                if has(n, 3):
                    wait(act, s["x1_mm"], n - 3)
                    act.wait_ge(s["tokt_mm"], n - 2)
                    nc.scalar.activation(mixed_t[:], x0[:, 0:S], ACT.Copy).then_inc(s["tokt_read"], 1)
                if has(n, 0):
                    unit(n, 1)
                if has(n, 1):
                    wait(act, s["q_mm"], n - 1)
                    act.wait_ge(slot_used[1], n)
                    nc.scalar.activation(y[:], y_bank[:, 0:S], ACT.Copy).then_inc(s["y_read"], 1)
                if has(n, 2):
                    act.wait_ge(s["sub_done"], n - 1)
                    nc.scalar.activation(prob[:], score[:], ACT.Exp, scale=float(DH) ** -0.5).then_inc(s["exp_done"], 1)
                if has(n, 0):
                    unit(n, 2)
                if has(n, 3):
                    wait(act, s["logit_mm"], n - 3)
                    act.wait_ge(s["t_mm"], n - 2)
                    nc.scalar.activation(t_t[:], x0[:, 0:S], ACT.Identity, bias=const("bbase")).then_inc(s["t_read"], 1)
                if has(n, 1):
                    wait(act, s["v_mm"], n - 1)
                    act.wait_ge(s["lat_mm"], n)
                    nc.scalar.activation(lat[0:LAT, :], x2[0:LAT, 0:S], ACT.Identity, bias=const("bdown", LAT))\
                        .then_inc(s["lat_read"], 1)
                if has(n, 3):
                    act.wait_ge(s["row_mm"], n - 2)
                    dst = rows[:].rearrange("p t r -> p (t r)")[:, bass.ds((n - 3) * 2 * ROW, 2 * ROW)]
                    nc.scalar.activation(dst.rearrange("p (t r) -> p t r", t=2)[:, :, 0:2 * D],
                                         x1[:].rearrange("p (t r) -> p t r", t=2), ACT.Copy).then_inc(s["row_read"], 1)
                if has(n, 0):
                    high(n, 1)
                    unit(n, 3)
                    unit(n, 4)
                if has(n, 1):
                    wait(act, s["pv_prod_done"], 2 * (n - 1))
                    act.wait_ge(s["v_mm"], n)
                    nc.scalar.activation(v[:].rearrange("p t d g -> p t g d"),
                                         x2[:, 0:2 * D].rearrange("p (t g d) -> p t g d", t=2, d=DH),
                                         ACT.Copy).then_inc(s["v_read"], 1)
                if has(n, 0):
                    unit(n, 5)

            pipeline(act, step)

            act.wait_ge(rr, 2)
            nc.scalar.activation(l_exp[:], l_exp[:], ACT.Exp).then_inc(rr_exp, 1)

            def ffn_gelu(i, o):
                t, q, par = at(i, o), o % RING, o % 2
                act.wait_ge(hot_done, t + 1)
                wait(act, fy_mm, t - 1)
                act.wait_ge(h_mm, t + 1)
                for k in range(FC):
                    ins = nc.scalar.activation(fh[par][:, k, :], h_bank[par][:, k * 128:(k + 1) * 128],
                                               ACT.Gelu_apprx_tanh, bias=hot[q % 4][:, F + k:F + k + 1])
                ins.then_inc(h_done, 1)

            tiles(act, LEAD, SLOT_TILES, ffn_gelu)

        @block.tensor
        def _(pe):
            def gate_up(b, n):
                k, half = UNITS[n]
                if half == 0:
                    turn = b if k < 2 else 0
                    pe.wait_ge(gu_hi_done[k], turn + 1)
                    pe.wait_ge(gu_lo_done[k], turn + 1)
                wait(pe, hid_done, b * NU + n - 1)
                cols = bass.ds(b * S, S)
                for dst, base in ((g_bank[n % 2], 0), (u_bank[n % 2], F)):
                    for j in (0, 1):
                        a = base + (2 * half + j) * 128
                        o = dst[:, j * S:(j + 1) * S]
                        pe.matmul(o, gu_hi[k][:, a:a + 128], xt_hi[:, cols], start=True, stop=False)
                        pe.matmul(o, gu_hi[k][:, a:a + 128], xt_lo[:, cols], start=False, stop=False)
                        last = pe.matmul(o, gu_lo[k][:, a:a + 128], xt_hi[:, cols], start=False, stop=True)
                last.then_inc(gu_mm, 1)

            def down_proj(b, n):
                k, half = UNITS[n]
                pe.wait_ge(hid_done, b * NU + n + 1)
                if half == 0:
                    turn = b if k < 2 else 0
                    pe.wait_ge(down_in[k], 16 * (turn + 1))
                if n == 0:
                    wait(pe, s["y_read"], b)
                for j in (0, 1):
                    ch = 2 * half + j
                    last = pe.matmul(y_bank[:, 0:S], down[k][:, ch * 128:(ch + 1) * 128], hid[:, n % 3, j * S:(j + 1) * S],
                                     start=(n == 0 and j == 0), stop=(n == NU - 1 and j == 1))
                last.then_inc(slot_used[k] if half else down_mm, 1)


            def effective_weights():
                pe.wait_ge(const_in, 16)
                pe.wait_ge(lora_done, B)
                for j, to in ((0, x0), (1, x1)):
                    pe.matmul(to[:], const("lora_a"), lora_scaled[:, 4 * j:4 * j + 4, :], start=True, stop=True)\
                        .then_inc(eff_mm, 1)

            def step(n):
                if has(n, 0):
                    if isinstance(n, int) and n < 2:
                        pe.wait_ge(x_hi_done, n + 1)
                        pe.wait_ge(x_lo_done, n + 1)
                    gate_up(n, 0)
                    if isinstance(n, int) and n == 1:
                        effective_weights()
                if has(n, 1):
                    down_proj(n - 1, NU - 2)
                if has(n, 3):
                    pe.wait_ge(s["rope_read"], 2 * min(n - 1, B) if isinstance(n, int) else 2 * (n - 1))
                    wait(pe, s["logit_read"], n - 3)
                    pe.wait_ge(s["tok_done"], n - 2)
                    for j in (0, 1):
                        last = pe.transpose(x0[:, j * 128:(j + 1) * 128], mixed_tok[:, j, :], const("ident"))
                    last.then_inc(s["tokt_mm"], 1)
                if has(n, 0):
                    gate_up(n, 1)
                if has(n, 3):
                    pe.wait_ge(s["tokt_read"], n - 2)
                    pe.matmul(x1[:, 0:S], const("wout"), mixed_t[:], start=True, stop=True).then_inc(s["x1_mm"], 1)
                if has(n, 1):
                    down_proj(n - 1, NU - 1)
                if has(n, 0):
                    gate_up(n, 2)
                if has(n, 3):
                    pe.wait_ge(w_now_done, n - 2)
                    pe.wait_ge(s["x1_made"], n - 2)
                    pe.matmul(x0[:, 0:S], w_now[:], x1_t[:], start=True, stop=True).then_inc(s["t_mm"], 1)
                if has(n, 0):
                    down_proj(n, 0)
                if has(n, 1):
                    if isinstance(n, int) and n == 1:
                        pe.wait_ge(eff_done, 2)
                        pe.wait_ge(ones_set, 4)
                        pe.wait_ge(bias_placed, 48)
                    pe.wait_ge(s["y_read"], n)
                    wait(pe, s["v_read"], n - 1)
                    pe.matmul(x2[0:LAT, 0:S], const("wdown"), y[:], start=True, stop=True).then_inc(s["lat_mm"], 1)
                if has(n, 3):
                    pe.wait_ge(s["t_read"], n - 2)
                    for j in (0, 1):
                        pe.transpose(x1[:, j * 2 * D:j * 2 * D + D], t_t[:, j * 128:(j + 1) * 128], const("ident"))
                        last = pe.transpose(x1[:, j * 2 * D + D:j * 2 * D + 2 * D], x1_t[:, j * 128:(j + 1) * 128], const("ident"))
                    last.then_inc(s["row_mm"], 1)
                if has(n, 0):
                    gate_up(n, 3)
                if has(n, 1):
                    wait(pe, s["rope_read"], 2 * (n - 1))
                    if has(n, 3):
                        pe.wait_ge(s["row_read"], n - 2)
                    for i, (to, w) in enumerate(((x0, "wq"), (x1, "wq_swap"))):
                        pe.matmul(to[:], ones_b[0:3, :], bias_rows[:, 4 * D * i:4 * D * (i + 1)], start=True, stop=False,
                                  skip_group_check=True)
                        for j in (0, 1):
                            last = pe.matmul(to[:, j * 2 * D:j * 2 * D + D], y[:, j * 128:(j + 1) * 128], const(w),
                                             start=False, stop=False, skip_group_check=True)
                    last.then_inc(s["q_mm"], 1)
                if has(n, 0):
                    down_proj(n, 1)
                if has(n, 1):
                    pe.wait_ge(s["lat_read"], n)
                    for to, w in ((x0, "wk"), (x1, "wk_swap")):
                        for j in (0, 1):
                            last = pe.matmul(to[:, j * 2 * D + D:j * 2 * D + 2 * D], lat[:, j * 128:(j + 1) * 128],
                                             const(w, LAT + 1), start=False, stop=True, skip_group_check=True)
                    last.then_inc(s["k_mm"], 1)
                    for j in (0, 1):
                        last = pe.matmul(x2[:, j * D:(j + 1) * D], lat[:, j * 128:(j + 1) * 128], const("wv", LAT + 1),
                                         start=True, stop=True)
                    last.then_inc(s["v_mm"], 1)
                if has(n, 0):
                    gate_up(n, 4)
                    down_proj(n, 2)
                    gate_up(n, 5)
                    down_proj(n, 3)
                if has(n, 3):
                    pe.wait_ge(s["rope_read"], 2 * min(n, B) if isinstance(n, int) else 2 * n)
                    for j in (0, 1):
                        last = pe.matmul(x0[:, j * E:(j + 1) * E], t_t[:, j * 128:(j + 1) * 128], const("switch_w"),
                                         start=True, stop=True)
                    last.then_inc(s["logit_mm"], 1)

            pipeline(pe, step)

            pe.wait_ge(rr, 6)
            pe.matmul(x1[:, 0:TT * E], earlier_b[:], onehot_b[:], start=True, stop=True)
            pe.matmul(x1[:, TT * E:2 * TT * E], ones_b[:], onehot_b[:], start=True, stop=True).then_inc(count_mm, 1)

            def slots_t(i, o):
                t, q = at(i, o), o % RING
                wait(pe, st_done, t - 1)
                pe.wait_ge(row_in[q], fills(i, o))
                pe.transpose(st_bank[q % 2][:, 0:128], srow[q][:, 0:D], const("ident")).then_inc(st_mm, 1)

            def ffn_h(i, o):
                t, q = at(i, o), o % RING
                pe.wait_ge(hot_done, t + 1)
                wait(pe, h_done, t - 1)
                pe.wait_ge(st_done, t + 1)
                for k in range(FC):
                    last = pe.matmul(h_bank[q % 2][:, k * 128:(k + 1) * 128], hot[q % 4][:, k * 128:(k + 1) * 128], st[q % 2],
                                     start=True, stop=True)
                last.then_inc(h_mm, 1)

            def ffn_y(i, o):
                t, q = at(i, o), o % RING
                e = pe.value_load(owner[0:1, bass.ds(t, 1)], min_val=0, max_val=E - 1)
                wait(pe, y1_done, t - 1)
                pe.wait_ge(h_done, t + 1)
                w2 = fw[:, bass.ds(e, 1), HOT_W:].rearrange("p a w -> p (a w)")
                for k in range(FC):
                    last = pe.matmul(fy_bank[q % 2][:, 0:D], fh[q % 2][:, k, :], w2[:, k * D:(k + 1) * D],
                                     start=(k == 0), stop=(k == FC - 1))
                last.then_inc(fy_mm, 1)

            def ffn_tile(i, o):
                if not (isinstance(i, int) and o < 2):
                    ffn_h(i, o - 2)
                if not (isinstance(i, int) and o < 3):
                    ffn_y(i, o - 3)
                if not (isinstance(i, int) and o >= SLOT_TILES):
                    slots_t(i, o)

            pe.wait_ge(rr_owner, 1)
            pe.wait_ge(ffn_in, 16 * E)
            tiles(pe, LEAD, SLOT_TILES, ffn_tile)
            ffn_tile(0, SLOT_TILES)
            ffn_tile(0, SLOT_TILES + 1)
            ffn_y(0, SLOT_TILES - 1)

        @block.vector
        def _(dve):
            done = [0]

            def chain(ins):
                done[0] += 1
                ins.then_inc(rt, 1)
                dve.wait_ge(rt, done[0])

            dve.wait_ge(cond_in, 16)
            chain(nc.vector.reduce_max(r_max[:], cb[:], AX))
            chain(nc.vector.tensor_tensor(r_exp[:], cb[:], r_max[:].unsqueeze(2).broadcast_to([128, B, E]), ALU.subtract))
            dve.wait_ge(r_expd, 1)
            chain(nc.vector.reduce_sum(r_sum[:], r_exp[:], AX))
            chain(nc.vector.reciprocal(r_sum[:], r_sum[:]))
            chain(nc.vector.tensor_tensor(r_prob[:], r_exp[:], r_sum[:].unsqueeze(2).broadcast_to([128, B, E]), ALU.mult))
            for b in range(B):
                ins = nc.vector.max(r_top[:, b, :], r_prob[:, b, :])
            chain(ins)
            for b in range(B):
                ins = nc.vector.max_index(chosen[:, b, :], r_top[:, b, :], r_prob[:, b, :])
            ins.then_inc(chosen_done, 1)
            chain(nc.vector.reduce_sum(r_norm[:], r_top[:, :, 0:TOP_K], AX))
            chain(nc.vector.reciprocal(r_norm[:], r_norm[:]))
            chain(nc.vector.tensor_tensor(r_w[:], r_top[:, :, 0:TOP_K], r_norm[:].unsqueeze(2).broadcast_to([128, B, TOP_K]),
                                          ALU.mult))
            chain(nc.vector.tensor_scalar(r_part[:], r_w[:], 1.0 - 1.0 / MOE_LAYERS, None, ALU.mult))
            chain(nc.vector.scalar_tensor_tensor(weight[:, :, 0:TOP_K], r_w[:], 1.0 / MOE_LAYERS, r_part[:], ALU.mult, ALU.add))
            nc.vector.memset(weight[:, :, TOP_K:TOP_K + 1], 1.0).then_inc(weight_done, 1)
            dve.wait_ge(weight_done, 1)

            def split_x(i, a, end):
                dve.wait_ge(x_in[i], 16)
                nc.vector.tensor_copy(xt_hi[:, a:end], xt[:, a:end]).then_inc(x_hi_done, 1)
                dve.wait_ge(x_hi_done, i + 1)
                nc.vector.tensor_tensor(xt_lo[:, a:end], xt[:, a:end], xt_hi[:, a:end].bitcast(F32), ALU.subtract)\
                    .then_inc(x_lo_done, 1)

            weights = weight[:].rearrange("p b k -> p (b k)")

            def unit(b, n):
                k, half = UNITS[n]
                dve.wait_ge(gelu_done, b * NU + n + 1)
                if half == 0:
                    pk, turn = UNITS[(n - 3) % NU][0], (b if n >= 3 else b - 1)
                    wait(dve, slot_used[pk], turn + 1)
                else:
                    wait(dve, down_mm, b * (NU // 2) + (n - 3) // 2 + 1)
                nc.vector.scalar_tensor_tensor(hid[:, n % 3, :], u_bank[n % 2], weights[:, bass.ds(b * (TOP_K + 1) + k, 1)],
                                               gelu[:, n % 2, :], ALU.mult, ALU.mult).then_inc(hid_done, 1)


            def effective_weights():
                dve.wait_ge(bias_in, 16)
                nc.vector.tensor_copy(bias_split[:, 0, :], bias_in_f[:]).then_inc(bias_done, 1)
                dve.wait_ge(bias_done, 1)
                chain(nc.vector.tensor_tensor(bias_rest[:], bias_in_f[:], bias_split[:, 0, :], ALU.subtract))
                nc.vector.tensor_copy(bias_split[:, 1, :], bias_rest[:]).then_inc(bias_done, 1)
                dve.wait_ge(bias_done, 2)
                nc.vector.tensor_tensor(bias_split[:, 2, :], bias_rest[:], bias_split[:, 1, :], ALU.subtract)\
                    .then_inc(bias_done, 1)

                dve.wait_ge(const_in, 16)
                for b in range(B):
                    cond_b = const("cond_rows")[:, b:b + 1]
                    nc.vector.tensor_scalar(lora_scaled[:, b, :], const("lora_b"), cond_b, 2.0, ALU.mult, ALU.mult)\
                        .then_inc(lora_done, 1)

            def effective_sum():
                for j, of in ((0, x0), (1, x1)):
                    dve.wait_ge(eff_mm, j + 1)
                    nc.vector.tensor_tensor(w_eff[:, 4 * j:4 * j + 4, :], of[:].rearrange("p (b o) -> p b o", b=4),
                                            const("wbase").unsqueeze(1).broadcast_to([128, 4, D]), ALU.add).then_inc(eff_done, 1)
                dve.wait_ge(eff_done, 2)

            split_x(0, 0, S)

            def step(n):
                if has(n, 0):
                    unit(n, 0)
                if has(n, 2):
                    qk_sum(n - 1, 1)
                    dve.wait_ge(s["score_done"], 2 * (n - 1))
                    nc.vector.reduce_max(s_max[:], score[:], AX).then_inc(s["max_done"], 1)
                    dve.wait_ge(s["max_done"], n - 1)
                    nc.vector.tensor_tensor(score[:], score[:], s_max[:].unsqueeze(3).broadcast_to([128, 2, NH, NH]),
                                            ALU.subtract).then_inc(s["sub_done"], 1)
                if has(n, 3):
                    nc.vector.tensor_copy(w_now[:], w_eff[:].rearrange("p b o -> p (b o)")[:, bass.ds((n - 3) * D, D)])\
                        .then_inc(w_now_done, 1)
                    dve.wait_ge(s["x1_mm"], n - 2)
                    nc.vector.scalar_tensor_tensor(x1_t[:], x1[:, 0:S], const("bout"), xt[:, bass.ds((n - 3) * S, S)],
                                                   ALU.add, ALU.add).then_inc(s["x1_made"], 1)
                if has(n, 0):
                    unit(n, 1)
                    if isinstance(n, int) and n == 0:
                        split_x(1, S, T)
                    if isinstance(n, int) and n == 1:
                        effective_sum()
                if has(n, 2):
                    dve.wait_ge(s["exp_done"], n - 1)
                    nc.vector.reduce_sum(den[:], prob[:], AX).then_inc(s["sum_done"], 1)
                if has(n, 0):
                    unit(n, 2)
                if has(n, 2):
                    dve.wait_ge(s["sum_done"], n - 1)
                    nc.vector.reciprocal(den[:], den[:]).then_inc(s["recip_done"], 1)
                    values_sum(n, 0)
                if has(n, 0):
                    unit(n, 3)
                if has(n, 1):
                    dve.wait_ge(s["k_mm"], n)
                    for i, (of, table) in enumerate(((x0, "cos"), (x1, "sin"))):
                        nc.vector.tensor_tensor(rope[:, i, :], of[:], const(table), ALU.mult).then_inc(s["rope_read"], 1)
                    dve.wait_ge(s["rope_read"], 2 * n)
                    nc.vector.tensor_tensor(qk[:].rearrange("p t j h d -> p (t j h d)"), rope[:, 0, :], rope[:, 1, :],
                                            ALU.add).then_inc(s["turned"], 1)
                    dve.wait_ge(s["turned"], n)
                    nc.vector.tensor_tensor(qk_prod[:, 0], qk[:, 0, 0].unsqueeze(2).broadcast_to([128, NH, NH, DH]),
                                            qk[:, 0, 1].unsqueeze(1).broadcast_to([128, NH, NH, DH]), ALU.mult)\
                        .then_inc(s["qk_prod_done0"], 1)
                if has(n, 0):
                    unit(n, 4)
                if has(n, 3):
                    dve.wait_ge(s["logit_mm"], n - 2)
                    dst = logit[:].rearrange("p t e -> p (t e)")[:, bass.ds((n - 3) * 2 * E, 2 * E)]
                    nc.vector.tensor_tensor(dst.rearrange("p (t e) -> p t e", e=E),
                                            x0[:, 0:2 * E].rearrange("p (t e) -> p t e", e=E),
                                            const("switch_b").unsqueeze(1).broadcast_to([128, 2, E]), ALU.add)\
                        .then_inc(s["logit_read"], 1)
                if has(n, 2):
                    values_sum(n, 1)
                    dve.wait_ge(s["recip_done"], n - 1)
                    dve.wait_ge(s["pv_done"], 2 * (n - 1))
                    wait(dve, s["tokt_mm"], n - 2)
                    nc.vector.tensor_tensor(mixed_tok[:].rearrange("p t (h d) -> p t h d", d=DH), mixed[:],
                                            den[:].unsqueeze(3).broadcast_to([128, 2, NH, DH]), ALU.mult)\
                        .then_inc(s["tok_done"], 1)
                if has(n, 0):
                    unit(n, 5)
                    if isinstance(n, int) and n == 0:
                        effective_weights()
                if has(n, 1):
                    qk_sum(n, 0)

            def values_sum(n, tile):
                dve.wait_ge(s["pv_prod_done"], 2 * (n - 2) + tile + 1)
                nc.vector.reduce_sum(mixed[:, tile], pv_prod[:, tile], AX).then_inc(s["pv_done"], 1)

            def qk_sum(n, tile):
                dve.wait_ge(s[f"qk_prod_done{tile}"], n)
                if tile == 0:
                    wait(dve, s["exp_done"], n - 1)
                nc.vector.reduce_sum(score[:, tile], qk_prod[:, tile], AX).then_inc(s["score_done"], 1)

            pipeline(dve, step)

            steps = [0]

            def link(ins):
                steps[0] += 1
                ins.then_inc(rr, 1)
                dve.wait_ge(rr, steps[0])

            def over_experts(ap):
                return ap.unsqueeze(2).broadcast_to([128, TT, E])

            dve.wait_ge(s["logit_read"], B)
            link(nc.vector.reduce_max(l_max[:], logit[:], AX))
            link(nc.vector.tensor_tensor(l_exp[:], logit[:], over_experts(l_max[:]), ALU.subtract))
            dve.wait_ge(rr_exp, 1)
            link(nc.vector.scalar_tensor_tensor(l_eq[:], l_exp[:], 1.0, const("falling").unsqueeze(1).broadcast_to([128, TT, E]),
                                                ALU.is_ge, ALU.mult))
            link(nc.vector.reduce_max(l_first[:], l_eq[:], AX))
            link(nc.vector.tensor_tensor(onehot[:], l_eq[:], over_experts(l_first[:]), ALU.is_equal))
            nc.vector.tensor_copy(earlier_b[:], const("earlier_row"))
            link(nc.vector.tensor_copy(onehot_b[:], onehot[:].rearrange("p t e -> p (t e)")))
            link(nc.vector.reduce_sum(l_sum[:], l_exp[:], AX))
            dve.wait_ge(s["row_read"], B)
            dve.wait_ge(ids_in, 16)
            nc.vector.reciprocal(rows[:, :, PROB], l_sum[:]).then_inc(rr_cols, 1)
            nc.vector.tensor_copy(rows[:, :, IDX].bitcast(I32), ids[:]).then_inc(rr_cols, 1)
            dve.wait_ge(count_mm, 1)
            link(nc.vector.tensor_copy(total[:], x1[:, TT * E:2 * TT * E].rearrange("p (t e) -> p t e", e=E)))
            src, k, shift = total, 0, 1
            while shift < TT:
                dst = scan[k % 2]
                nc.vector.tensor_copy(dst[:, 0:shift, :], src[:, 0:shift, :])
                link(nc.vector.tensor_tensor(dst[:, shift:, :], src[:, shift:, :], src[:, 0:TT - shift, :], ALU.add))
                src, k, shift = dst, k + 1, 2 * shift
            link(nc.vector.tensor_tensor(over[:], src[:, TT - 1, :].unsqueeze(2).broadcast_to([128, E, TT]),
                                         const("ramp").unsqueeze(1).broadcast_to([128, E, TT]), ALU.is_gt))
            link(nc.vector.reduce_sum(n_tiles[:], over[:], AX))
            link(nc.vector.tensor_tensor(prev_tiles[:], n_tiles[:].unsqueeze(1).broadcast_to([128, E, E]),
                                         const("before").rearrange("p (a b) -> p a b", a=E), ALU.mult))
            link(nc.vector.reduce_sum(first_tile[:], prev_tiles[:], AX))
            link(nc.vector.tensor_tensor(end_tile[:], first_tile[:], n_tiles[:], ALU.add))
            link(nc.vector.tensor_tensor(place[:], src[:], total[:], ALU.subtract))
            link(nc.vector.tensor_tensor(place[:], x1[:, 0:TT * E].rearrange("p (t e) -> p t e", e=E), place[:], ALU.add))
            link(nc.vector.scalar_tensor_tensor(place[:], first_tile[:].unsqueeze(1).broadcast_to([128, TT, E]), 128.0, place[:],
                                                ALU.mult, ALU.add))
            link(nc.vector.tensor_tensor(place[:], place[:], onehot[:], ALU.mult))
            link(nc.vector.reduce_sum(slot_f[:], place[:], AX))
            nc.vector.tensor_copy(slot[:], slot_f[:]).then_inc(rr_slot, 1)
            link(nc.vector.tensor_tensor(ended[:], end_tile[:].unsqueeze(1).broadcast_to([128, SLOT_TILES, E]),
                                         const("slot_tile").unsqueeze(2).broadcast_to([128, SLOT_TILES, E]), ALU.is_le))
            link(nc.vector.reduce_sum(owner_f[:], ended[:], AX))
            nc.vector.tensor_scalar(owner[:], owner_f[:], float(E - 1), None, ALU.min).then_inc(rr_owner, 1)

            def ffn_hot(i, o):
                t, q = at(i, o), o % RING
                e = dve.value_load(owner[0:1, bass.ds(t, 1)], min_val=0, max_val=E - 1)
                nc.vector.tensor_copy(hot[q % 4], fw[:, bass.ds(e, 1), 0:HOT_W].rearrange("p a w -> p (a w)"))\
                    .then_inc(hot_done, 1)

            def ffn_st(i, o):
                t, q = at(i, o), o % RING
                wait(dve, h_mm, t - 1)
                dve.wait_ge(st_mm, t + 1)
                nc.vector.tensor_copy(st[q % 2], st_bank[q % 2][:, 0:128]).then_inc(st_done, 1)

            def ffn_y1(i, o):
                t, q = at(i, o), o % RING
                wait(dve, z_done, t - 1)
                dve.wait_ge(fy_mm, t + 1)
                nc.vector.tensor_tensor(y1[q % 2], fy_bank[q % 2][:, 0:D], hot[q % 4][:, F + FC:], ALU.add).then_inc(y1_done, 1)

            def ffn_z(i, o):
                t, q = at(i, o), o % RING
                wait(dve, yo_done, t - 1)
                dve.wait_ge(y1_done, t + 1)
                nc.vector.tensor_scalar(z[q % 2], y1[q % 2], srow[q][:, PROB:PROB + 1], None, ALU.mult).then_inc(z_done, 1)

            def ffn_tile(i, o):
                if not (isinstance(i, int) and o < 3):
                    ffn_y1(i, o - 3)
                if not (isinstance(i, int) and o >= SLOT_TILES):
                    ffn_st(i, o)
                if not (isinstance(i, int) and o < 3):
                    ffn_z(i, o - 3)
                if not (isinstance(i, int) and o >= SLOT_TILES):
                    ffn_hot(i, o)

            dve.wait_ge(ffn_in, 16 * E)
            dve.wait_ge(rr_owner, 1)
            tiles(dve, LEAD, SLOT_TILES, ffn_tile)
            for t in range(SLOT_TILES, SLOT_TILES + 3):
                ffn_tile(0, t)


def kernel(**inputs):
    import numpy as np
    import concourse.bacc as bacc
    from concourse.bass_utils import run_bass_kernel_spmd

    a = {k: np.asarray(val) for k, val in inputs.items()}
    x_t = np.ascontiguousarray(a["x"].reshape(T, D).T)

    def chunked(w):
        return w.reshape(*w.shape[:-2], FC, 128, D).swapaxes(-3, -2).reshape(*w.shape[:-2], 128, FC * D)

    skill = np.concatenate([a["L0_cond_skill_gate"], a["L0_cond_skill_up"], chunked(a["L0_cond_skill_down"])], axis=2)
    shared = np.concatenate([a["L0_cond_shared_gate"], a["L0_cond_shared_up"], chunked(a["L0_cond_shared_down"])], axis=1)
    experts = np.ascontiguousarray(np.concatenate([skill, shared[None]], axis=0))
    ffn = np.ascontiguousarray(np.concatenate([
        a["L0_ffn_w1"], a["L0_ffn_b1"].reshape(E, FC, 128).swapaxes(1, 2),
        np.broadcast_to(a["L0_ffn_b2"][:, None, :], (E, 128, D)), chunked(a["L0_ffn_w2"])], axis=2))
    cond = np.ascontiguousarray(np.broadcast_to(a["cond_8"].reshape(1, B * E), (128, B * E)))

    pos = np.arange(S, dtype=np.float32)
    freq = (1.0 / np.float32(10000.0) ** (np.arange(0, DH, 2, dtype=np.float32) / DH)).astype(np.float32)
    angle = (pos[:, None] * freq[None, :]).astype(np.float32)
    half = DH // 2
    feature = np.arange(D)
    sign = np.where(feature % DH < half, -1, 1).astype(np.float32)
    cos = np.tile(np.cos(angle).astype(np.float32)[:, feature % half].reshape(2, 128, 1, D), (1, 1, 2, 1))
    sin = np.tile((np.sin(angle).astype(np.float32)[:, feature % half] * sign).reshape(2, 128, 1, D), (1, 1, 2, 1))
    cos, sin = (a_.transpose(1, 0, 2, 3).reshape(128, 4 * D) for a_ in (cos, sin))
    swap = (feature // DH) * DH + (feature % DH + half) % DH
    k_cols = (feature // DH) * 2 * DH + feature % DH
    up = np.concatenate([a["L0_attn_Wup"], a["L0_attn_bup"][None]], axis=0)
    order = np.arange(128)
    r = a["L0_cond2_As"].shape[1]
    full = {
        "switch_b": np.broadcast_to(a["L0_ffn_switch_b"][None], (128, E)),
        "cond_rows": np.repeat(a["cond_8"].T, r, axis=0),
        "wq": a["L0_attn_Wq"], "wq_swap": a["L0_attn_Wq"][:, swap],
        "wk": up[:, k_cols], "wk_swap": up[:, k_cols[swap]], "wv": up[:, k_cols + DH],
        "wdown": a["L0_attn_Wdown"],
        "bdown": a["L0_attn_bdown"][:, None], "wout": a["L0_attn_Wout"], "bout": a["L0_attn_bout"][:, None],
        "wbase": a["L0_cond2_W_base"].T, "bbase": a["L0_cond2_b_base"][:, None],
        "lora_a": a["L0_cond2_As"].reshape(E * r, D), "lora_b": a["L0_cond2_Bs"].swapaxes(1, 2).reshape(E * r, D),
        "switch_w": a["L0_ffn_switch_w"], "cos": cos, "sin": sin, "ident": np.eye(128, dtype=np.float32),
        "earlier_row": (order[:, None] < order[None, :]).astype(np.float32),
        "falling": np.broadcast_to(np.arange(E, 0, -1, dtype=np.float32), (128, E)),
        "ramp": np.broadcast_to(128 * np.arange(TT, dtype=np.float32), (128, TT)),
        "before": np.broadcast_to((np.arange(E)[None, :] < np.arange(E)[:, None]).astype(np.float32).reshape(1, E * E),
                                  (128, E * E)),
        "slot_tile": np.broadcast_to(np.arange(SLOT_TILES, dtype=np.float32), (128, SLOT_TILES)),
    }
    consts = np.zeros((128, CONST_W), np.float32)
    for name, (at, width) in AT.items():
        consts[:full[name].shape[0], at:at + width] = full[name]
    query_bias = np.zeros((2, 2, 2, D), np.float32)
    query_bias[0, :, 0], query_bias[1, :, 0] = a["L0_attn_bq"], a["L0_attn_bq"][swap]
    query_bias = query_bias.reshape(1, 8 * D)
    token_ids = np.ascontiguousarray(np.arange(T, dtype=np.int32).reshape(TT, 128).T)

    arrays = {"in_x_t": x_t, "in_cond": cond, "in_experts": experts, "in_ffn": ffn, "in_consts": consts, "in_query_bias": query_bias,
              "in_token_ids": token_ids}
    nc = bacc.Bacc("TRN2", target_bir_lowering=False, num_devices=1)
    args = [nc.dram_tensor(name, v.shape, mybir.dt.from_np(v.dtype), kind="ExternalInput").ap() for name, v in arrays.items()]
    out = nc.dram_tensor("out", (T, D), F32, kind="ExternalOutput").ap()
    adaln_program(nc, *args, out)
    r = run_bass_kernel_spmd(nc, [arrays], core_ids=[0])
    return r.results[0]["out"].reshape(B, S, D)
```

```python
from contextlib import ExitStack

import concourse.bass as bass
from concourse import mybir

F32 = mybir.dt.float32
F32R = mybir.dt.float32r
BF16 = mybir.dt.bfloat16
U32 = mybir.dt.uint32
I32 = mybir.dt.int32
ACT = mybir.ActivationFunctionType
ALU = mybir.AluOpType
AX = mybir.AxisListType.X

B, S, D = 8, 256, 128
T = B * S
E, F = 8, 512
NH, DH = 16, 8
LAT = 32
TOP_K, MOE_LAYERS = 2, 12
FC = F // 128
TT = T // 128
SLOT_TILES = TT + E - 1
REGION = T + 128
SLOTS = E * REGION + 128
ROUTES = ((0, TT - 4), (TT - 4, TT - 2), (TT - 2, TT))
PROB, IDX, ROW = 2 * D, 2 * D + 1, 2 * D + 2
NO_TOKEN = 1 << 20
RING = 8
HOT_AHEAD = 3
OWNED = SLOT_TILES + HOT_AHEAD
LEAD = SLOT_TILES % RING
HOT_W = F + FC + D
FFN_W = HOT_W + F

FIELDS = [("switch_b", E), ("cond_rows", B), ("wq", D), ("wq_swap", D), ("wk", D), ("wk_swap", D), ("wv", D),
          ("wdown", LAT), ("bdown", 1), ("wout", D), ("bout", 1), ("wbase", D),
          ("bbase", 1), ("lora_a", D), ("lora_b", D), ("switch_w", E), ("cos", 4 * D), ("sin", 4 * D), ("ident", D),
          ("earlier_row", D), ("falling", E), ("region", E), ("ramp", E * TT), ("up_to", E * E), ("slot_tile", OWNED)]
AT, CONST_W = {}, 0
for _name, _width in FIELDS:
    AT[_name] = (CONST_W, _width)
    CONST_W += _width


def adaln_program(nc, x_t, cond, experts, ffn, consts, query_bias, token_ids, out):
    ctx = ExitStack()
    with ctx:
        first = ctx.enter_context(ExitStack())

        def sb(name, shape, dt=F32, at=ctx):
            return at.enter_context(nc.sbuf_tensor(name, shape, dt))

        def sem(name):
            return ctx.enter_context(nc.semaphore(name))

        gu_bank = [ctx.enter_context(nc.psum_tensor(f"gu_bank{i}", [128, 2, 512], F32)) for i in (0, 1)]
        y_bank, x0, x1, x2 = [ctx.enter_context(nc.psum_tensor(n, [128, 512], F32)) for n in ("y_bank", "x0", "x1", "x2")]

        slot_dram = nc.dram_tensor("slot_dram", [SLOTS, ROW], F32).ap()
        bias_dram = nc.dram_tensor("bias_dram", [3, 8, D], BF16).ap()

        gu, gu_hi, gu_lo, down = ([sb(f"{n}{k}", [128, w], dt, at=first) for k in range(3)] for n, w, dt in (
            ("gu", 2 * F, F32), ("gu_hi", 2 * F, F32R), ("gu_lo", 2 * F, F32R), ("down", F, F32)))
        first.close()
        fw = sb("fw", [128, 3 * 7 * F])[:, 0:E * FFN_W].rearrange("p (e w) -> p e w", e=E)

        c = sb("c", [128, CONST_W])
        cb = sb("cb", [128, B, E])
        ids = sb("ids", [128, TT], I32)
        xt = sb("xt", [128, T])

        def const(name, rows=128):
            a, w = AT[name]
            return c[0:rows, a:a + w]

        r_max = sb("r_max", [128, B])
        r_exp = sb("r_exp", [128, B, E])
        r_sum = sb("r_sum", [128, B])
        r_prob = sb("r_prob", [128, B, E])
        r_top = sb("r_top", [128, B, 8])
        chosen = sb("chosen", [128, B, 8], U32)
        r_norm = sb("r_norm", [128, B])
        r_w = sb("r_w", [128, B, TOP_K])
        r_part = sb("r_part", [128, B, TOP_K])
        weight = sb("weight", [128, B, TOP_K + 1])

        xt_hi = sb("xt_hi", [128, T], F32R)
        xt_lo = sb("xt_lo", [128, T], F32R)
        gelu = sb("gelu", [128, 2, 512])
        hid = sb("hid", [128, 3, 512])

        lora_scaled = sb("lora_scaled", [128, B, D])
        w_eff = sb("w_eff", [128, B, D])
        w_now = sb("w_now", [128, D])
        bias_in_f = sb("bias_in_f", [8, D])
        bias_rest = sb("bias_rest", [8, D])
        bias_split = sb("bias_split", [8, 3, D], BF16)
        bias_rows = sb("bias_rows", [3, 8 * D], BF16)
        y = sb("y", [128, S])
        lat = sb("lat", [LAT + 1, S])
        rope = sb("rope", [128, 2, 4 * D])
        qk = sb("qk", [128, 2, 2, NH, DH])
        qk_prod = sb("qk_prod", [128, 2, NH, NH, DH])
        score = sb("score", [128, 2, NH, NH])
        s_max = sb("s_max", [128, 2, NH])
        prob = sb("prob", [128, 2, NH, NH])
        v = sb("v", [128, 2, DH, NH])
        pv_prod = sb("pv_prod", [128, 2, NH, DH, NH])
        mixed = sb("mixed", [128, 2, NH, DH])
        den = sb("den", [128, 2, NH])
        mixed_tok = sb("mixed_tok", [128, 2, D])
        mixed_t = sb("mixed_t", [128, S])
        x1_t = sb("x1_t", [128, S])
        t_t = sb("t_t", [128, S])
        rows = sb("rows", [128, TT, ROW])
        logit = sb("logit", [128, TT, E])

        l_max = sb("l_max", [128, TT])
        l_exp = sb("l_exp", [128, TT, E])
        l_sum = sb("l_sum", [128, TT])
        l_eq = sb("l_eq", [128, TT, E])
        l_first = sb("l_first", [128, TT])
        onehot = sb("onehot", [128, TT, E])
        onehot_b = sb("onehot_b", [128, TT * E], BF16)
        earlier_b = sb("earlier_b", [128, 128], BF16)
        ones_b = sb("ones_b", [128, 128], BF16)
        total = sb("total", [128, TT, E])
        scan = [sb(f"scan{i}", [128, TT, E]) for i in (0, 1)]
        over = sb("over", [128, E, TT])
        n_tiles = sb("n_tiles", [128, E])
        prev_tiles = sb("prev_tiles", [128, E, E])
        end_tile = sb("end_tile", [128, E])
        skip = sb("skip", [128, E])
        taken = sb("taken", [128, len(ROUTES) + 1, E])
        taken_u = sb("taken_u", [128, E], U32)
        place = sb("place", [128, TT, E])
        slot_f = sb("slot_f", [128, TT])
        slot = sb("slot", [128, TT], U32)
        ended = sb("ended", [128, OWNED, E])
        skipped = sb("skipped", [128, OWNED, E])
        source_f = sb("source_f", [128, OWNED])
        source = sb("source", [128, OWNED], U32)
        owner_f = sb("owner_f", [128, OWNED])
        owner = sb("owner", [128, OWNED], U32)
        empty = sb("empty", [128, ROW])

        srow = [pv_prod[:].rearrange("p a b c d -> p (a b c d)")[:, i * ROW:(i + 1) * ROW] for i in range(RING)]
        hot_at = [(qk_prod, i * HOT_W) for i in range(6)] + [(pv_prod, RING * ROW + i * HOT_W) for i in range(2)]
        hot = [t[:].rearrange("p a b c d -> p (a b c d)")[:, at_col:at_col + HOT_W] for t, at_col in hot_at]
        st = [hid[:, 2, i * 128:(i + 1) * 128] for i in (0, 1)]
        fh = [gelu[:, i, :].rearrange("p (k s) -> p k s", k=FC) for i in (0, 1)]
        y1 = [hid[:, i, 0:D] for i in (0, 1)]
        z = [hid[:, i, D:2 * D] for i in (0, 1)]

        cond_in, const_in, ids_in = sem("cond_in"), sem("const_in"), sem("ids_in")
        x_in = [sem("x_in_first"), sem("x_in_rest")]
        gu_in = [sem(f"gu_in{k}") for k in range(3)]
        down_in = [sem(f"down_in{k}") for k in range(3)]
        empty_out = sem("empty_out")
        rt, r_expd, chosen_done, weight_done = sem("rt"), sem("r_expd"), sem("chosen_done"), sem("weight_done")
        x_hi_done, x_lo_done = sem("x_hi_done"), sem("x_lo_done")
        gu_hi_done = [sem(f"gu_hi_done{k}") for k in range(3)]
        gu_lo_done = [sem(f"gu_lo_done{k}") for k in range(3)]
        slot_used = [sem(f"slot_used{k}") for k in range(3)]
        gu_mm, gelu_done, hid_done, down_mm = (
            sem(n) for n in ("gu_mm", "gelu_done", "hid_done", "down_mm"))
        lora_done, eff_mm, eff_done, w_now_done = sem("lora_done"), sem("eff_mm"), sem("eff_done"), sem("w_now_done")
        ones_set, bias_in, bias_done, bias_placed = sem("ones_set"), sem("bias_in"), sem("bias_done"), sem("bias_placed")
        bias_out = sem("bias_out")
        names = ("y_read lat_mm lat_read q_mm k_mm v_mm v_read rope_read turned qk_prod_done0 qk_prod_done1 "
                 "score_done max_done sub_done0 sub_done1 exp_done0 exp_done1 pv_prod_done0 pv_prod_done1 "
                 "pv_done sum_done recip_done tok_done tokt_mm tokt_read x1_mm x1_made t_mm t_read "
                 "row_mm row_read logit_mm logit_read")
        s = {n: sem(n) for n in names.split()}
        rr, rr_sub, rr_exp, rr_onehot, count_mm, rr_slot, rr_taken_f, rr_taken, rr_owner, rr_cols = (
            sem(n) for n in ("rr", "rr_sub", "rr_exp", "rr_onehot", "count_mm", "rr_slot", "rr_taken_f",
                             "rr_taken", "rr_owner", "rr_cols"))
        scattered, ffn_in, hot_done, st_mm, st_done, h_mm, h_done, fy_mm, y1_done, z_done, yo_done = (
            sem(n) for n in ("scattered", "ffn_in", "hot_done", "st_mm", "st_done", "h_mm", "h_done", "fy_mm",
                             "y1_done", "z_done", "yo_done"))
        row_in, stored = ([sem(f"{n}{i}") for i in range(RING)] for n in ("row_in", "stored"))

        def wait(eng, semaphore, value):
            if not (isinstance(value, int) and value <= 0):
                eng.wait_ge(semaphore, value)

        def at(i, o):
            return RING * i + o

        def fills(i, o):
            return 16 * (i + o // RING) + 16

        def tiles(eng, lead, end, body):
            for t in range(lead):
                body(0, t)
            with eng.Fori(0, (end - lead) // RING) as i:
                for j in range(RING):
                    body(i, lead + j)

        def pipeline(eng, step):
            for n in range(3):
                step(n)
            with eng.Fori(3, B) as n:
                step(n)
            for n in range(B, B + 3):
                step(n)

        def has(n, lag):
            return not isinstance(n, int) or 0 <= n - lag < B

        def mixes_on_dve(n):
            return isinstance(n, int) and n >= B

        UNITS = [(k, half) for k in (2, 0, 1) for half in (0, 1)]
        NU = len(UNITS)

        def used_by(b, k):
            return (b - 1) * NU + UNITS.index((k, 1)) + 1 if not (isinstance(b, int) and b == 0) else 0

        g_bank = [gu_bank[i][:, 0, :] for i in (0, 1)]
        u_bank = [gu_bank[i][:, 1, :] for i in (0, 1)]
        h_bank, st_bank, fy_bank = g_bank, [x0, x1], [x2, y_bank]

        def end_regions(eng, experts_of):
            eng.wait_ge(rr_taken, 1)
            for e in experts_of:
                end = eng.value_load(taken_u[0:1, e:e + 1], min_val=e * REGION, max_val=e * REGION + T)
                eng.dma_start(slot_dram[bass.ds(end, 128), :], empty[:]).then_inc(empty_out, 16)

        block = ctx.enter_context(nc.Block())

        @block.sync
        def _(sp):
            sp.dma_start(cb[:].rearrange("p b e -> p (b e)"), cond).then_inc(cond_in, 16)
            sp.dma_start(gu[2][:], experts[E, :, 0:2 * F]).then_inc(gu_in[2], 16)
            sp.dma_start(xt[:, 0:S], x_t[:, 0:S]).then_inc(x_in[0], 16)
            sp.dma_start(down[2][:], experts[E, :, 2 * F:3 * F]).then_inc(down_in[2], 16)
            sp.wait_ge(chosen_done, 1)

            def expert_load(b, k):
                e = sp.value_load(chosen[0:1, b, k:k + 1] if isinstance(b, int) else
                                  chosen[:].rearrange("p b e -> p (b e)")[0:1, bass.ds(b * 8 + k, 1)],
                                  min_val=0, max_val=E - 1)
                src = experts[bass.ds(e, 1)].rearrange("a p f -> p (a f)")
                wait(sp, gu_hi_done[k], b)
                wait(sp, gu_lo_done[k], b)
                sp.dma_start(gu[k][:], src[:, 0:2 * F]).then_inc(gu_in[k], 16)
                wait(sp, slot_used[k], b)
                sp.dma_start(down[k][:], src[:, 2 * F:3 * F]).then_inc(down_in[k], 16)

            expert_load(0, 0)
            expert_load(0, 1)
            sp.dma_start(xt[:, S:], x_t[:, S:]).then_inc(x_in[1], 16)
            sp.dma_start(c[:], consts).then_inc(const_in, 16)
            sp.dma_start(bias_in_f[:], query_bias).then_inc(bias_in, 16)
            sp.dma_start(ids[:], token_ids).then_inc(ids_in, 16)
            expert_load(1, 0)
            expert_load(1, 1)
            sp.wait_ge(bias_done, 3)
            for i in range(3):
                sp.dma_start(bias_dram[i], bias_split[:, i, :]).then_inc(bias_out, 16)
            sp.wait_ge(bias_out, 48)
            sp.dma_start(bias_rows[:], bias_dram.rearrange("i p d -> i (p d)")).then_inc(bias_placed, 16)
            sp.wait_ge(ones_set, 4)
            sp.dma_start(slot_dram[E * REGION:, :], empty[:]).then_inc(empty_out, 16)
            with sp.Fori(2, B) as b:
                expert_load(b, 0)
                expert_load(b, 1)

            sp.wait_ge(slot_used[1], B)
            for e in range(E):
                sp.dma_start(fw[:, e, :], ffn[e]).then_inc(ffn_in, 16)
            end_regions(sp, range(0, E, 2))
            sp.wait_ge(rr_owner, 2)
            sp.wait_ge(empty_out, 16 * (E + 1))
            sp.wait_ge(scattered, 16 * TT)

            for t in range(SLOT_TILES):
                wait(sp, stored[t % RING], fills(0, t - RING))
                at_slot = sp.value_load(source[0:1, t:t + 1], min_val=0, max_val=E * REGION)
                sp.dma_start(srow[t % RING], slot_dram[bass.ds(at_slot, 128), :]).then_inc(row_in[t % RING], 16)
            for t in range(SLOT_TILES - RING, SLOT_TILES):
                sp.wait_ge(stored[t % RING], fills(0, t))

        @block.gpsimd
        def _(pool):
            nc.gpsimd.memset(ones_b[:], 1.0).then_inc(ones_set, 1)
            nc.gpsimd.memset(lat[:], 1.0).then_inc(ones_set, 1)
            nc.gpsimd.memset(empty[:], 0.0).then_inc(ones_set, 1)
            pool.wait_ge(ones_set, 3)
            nc.gpsimd.memset(empty[:, IDX:IDX + 1].bitcast(I32), NO_TOKEN).then_inc(ones_set, 1)
            pool.wait_ge(ones_set, 4)

            def low(b, k):
                pool.wait_ge(gu_in[k], 16 * b + 16)
                pool.wait_ge(gu_hi_done[k], b + 1)
                wait(pool, gu_mm, used_by(b, k))
                nc.gpsimd.tensor_tensor(gu_lo[k][:], gu[k][:], gu_hi[k][:].bitcast(F32), ALU.subtract)\
                    .then_inc(gu_lo_done[k], 1)

            low(0, 2)

            def values(n, tile):
                pool.wait_ge(s["v_read"], n - 1)
                wait(pool, s["pv_done"], 2 * (n - 2) + tile - 1 if tile else 2 * (n - 2))
                pool.wait_ge(s[f"exp_done{tile}"], n - 1)
                nc.gpsimd.tensor_tensor(pv_prod[:, tile], prob[:, tile].unsqueeze(2).broadcast_to([128, NH, DH, NH]),
                                        v[:, tile].unsqueeze(1).broadcast_to([128, NH, DH, NH]), ALU.mult)\
                    .then_inc(s[f"pv_prod_done{tile}"], 1)

            def step(n):
                if has(n, 0):
                    low(n, 0)
                if has(n, 2):
                    values(n, 0)
                if has(n, 0):
                    low(n, 1)
                if has(n, 2) and not mixes_on_dve(n):
                    values(n, 1)
                if has(n, 1):
                    wait(pool, s["score_done"], 2 * (n - 1))
                    pool.wait_ge(s["turned"], n)
                    nc.gpsimd.tensor_tensor(qk_prod[:, 1], qk[:, 1, 0].unsqueeze(2).broadcast_to([128, NH, NH, DH]),
                                            qk[:, 1, 1].unsqueeze(1).broadcast_to([128, NH, NH, DH]), ALU.mult)\
                        .then_inc(s["qk_prod_done1"], 1)


            def scatter(r):
                a, b = ROUTES[r]
                pool.wait_ge(s["row_read"], b // 2)
                pool.wait_ge(rr_cols, r + 2)
                pool.wait_ge(rr_slot, r + 1)
                for i in range(a, b):
                    pool.indirect_dma_start(slot_dram, bass.IndirectOffsetOnAxis(slot[:, i:i + 1], 0),
                                            rows[:, i, :], None).then_inc(scattered, 16)

            pipeline(pool, step)
            for r in range(len(ROUTES)):
                scatter(r)

            def store(q):
                pool.indirect_dma_start(out, bass.IndirectOffsetOnAxis(srow[q][:, IDX:IDX + 1].bitcast(U32), 0),
                                        srow[q][:, D:2 * D], None, bounds_check=T - 1, oob_is_err=False)\
                    .then_inc(stored[q], 16)

            def add_x1(i, o):
                t, q = at(i, o), o % RING
                wait(pool, yo_done, t)
                pool.wait_ge(z_done, t + 1)
                nc.gpsimd.tensor_tensor(srow[q][:, D:2 * D], z[q % 2], srow[q][:, D:2 * D], ALU.add).then_inc(yo_done, 1)
                if not (isinstance(t, int) and t == 0):
                    store((q - 1) % RING)

            tiles(pool, LEAD, SLOT_TILES, add_x1)
            pool.wait_ge(yo_done, SLOT_TILES)
            store((SLOT_TILES - 1) % RING)
            for t in range(SLOT_TILES - RING, SLOT_TILES):
                pool.wait_ge(stored[t % RING], fills(0, t))

        @block.scalar
        def _(act):
            act.wait_ge(rt, 2)
            nc.scalar.activation(r_exp[:], r_exp[:], ACT.Exp).then_inc(r_expd, 1)

            def high(b, k):
                act.wait_ge(gu_in[k], 16 * b + 16)
                wait(act, gu_mm, used_by(b, k))
                nc.scalar.activation(gu_hi[k][:], gu[k][:], ACT.Copy).then_inc(gu_hi_done[k], 1)

            def unit(b, n):
                act.wait_ge(gu_mm, b * NU + n + 1)
                wait(act, hid_done, b * NU + n - 1)
                nc.scalar.activation(gelu[:, n % 2, :], g_bank[n % 2], ACT.Gelu_apprx_tanh).then_inc(gelu_done, 1)

            high(0, 2)

            def exponential(n, tile):
                act.wait_ge(s[f"sub_done{tile}"], n)
                nc.scalar.activation(prob[:, tile], score[:, tile], ACT.Exp, scale=float(DH) ** -0.5)\
                    .then_inc(s[f"exp_done{tile}"], 1)

            def route_exp(r):
                a, b = ROUTES[r]
                act.wait_ge(rr_sub, r + 1)
                nc.scalar.activation(l_exp[:, a:b, :], l_exp[:, a:b, :], ACT.Exp).then_inc(rr_exp, 1)

            def step(n):
                if has(n, 0):
                    high(n, 0)
                if isinstance(n, int) and n == 1:
                    act.wait_ge(const_in, 16)
                    act.wait_ge(ones_set, 4)
                if has(n, 0):
                    unit(n, 0)
                if has(n, 2):
                    exponential(n - 1, 0)
                if has(n, 3):
                    wait(act, s["x1_mm"], n - 3)
                    act.wait_ge(s["tokt_mm"], n - 2)
                    nc.scalar.activation(mixed_t[:], x0[:, 0:S], ACT.Copy).then_inc(s["tokt_read"], 1)
                if has(n, 0):
                    unit(n, 1)
                if has(n, 2):
                    exponential(n - 1, 1)
                if has(n, 1):
                    wait(act, s["q_mm"], n - 1)
                    act.wait_ge(slot_used[1], n)
                    nc.scalar.activation(y[:], y_bank[:, 0:S], ACT.Copy).then_inc(s["y_read"], 1)
                if isinstance(n, int) and n == B + 1:
                    route_exp(0)
                if has(n, 0):
                    high(n, 1)
                if has(n, 3):
                    wait(act, s["logit_mm"], n - 3)
                    act.wait_ge(s["t_mm"], n - 2)
                    nc.scalar.activation(t_t[:], x0[:, 0:S], ACT.Identity, bias=const("bbase")).then_inc(s["t_read"], 1)
                if has(n, 0):
                    unit(n, 2)
                if has(n, 3):
                    act.wait_ge(s["row_mm"], n - 2)
                    dst = rows[:].rearrange("p t r -> p (t r)")[:, bass.ds((n - 3) * 2 * ROW, 2 * ROW)]
                    nc.scalar.activation(dst.rearrange("p (t r) -> p t r", t=2)[:, :, 0:2 * D],
                                         x1[:].rearrange("p (t r) -> p t r", t=2), ACT.Copy).then_inc(s["row_read"], 1)
                if has(n, 1):
                    wait(act, s["v_mm"], n - 1)
                    act.wait_ge(s["lat_mm"], n)
                    nc.scalar.activation(lat[0:LAT, :], x2[0:LAT, 0:S], ACT.Identity, bias=const("bdown", LAT))\
                        .then_inc(s["lat_read"], 1)
                if isinstance(n, int) and n == B + 1:
                    route_exp(1)
                if has(n, 0):
                    unit(n, 3)
                    unit(n, 4)
                if has(n, 1):
                    wait(act, s["pv_prod_done0"], n - 1)
                    wait(act, s["pv_prod_done1"], n - 1)
                    act.wait_ge(s["v_mm"], n)
                    nc.scalar.activation(v[:].rearrange("p t d g -> p t g d"),
                                         x2[:, 0:2 * D].rearrange("p (t g d) -> p t g d", t=2, d=DH),
                                         ACT.Copy).then_inc(s["v_read"], 1)
                if has(n, 0):
                    unit(n, 5)

            pipeline(act, step)

            route_exp(2)
            end_regions(act, range(1, E, 2))

            def ffn_gelu(i, o):
                t, q, par = at(i, o), o % RING, o % 2
                act.wait_ge(hot_done, t + 1)
                wait(act, fy_mm, t - 1)
                act.wait_ge(h_mm, t + 1)
                for k in range(FC):
                    ins = nc.scalar.activation(fh[par][:, k, :], h_bank[par][:, k * 128:(k + 1) * 128],
                                               ACT.Gelu_apprx_tanh, bias=hot[q][:, F + k:F + k + 1])
                ins.then_inc(h_done, 1)

            tiles(act, LEAD, SLOT_TILES, ffn_gelu)

        @block.tensor
        def _(pe):
            def gate_up(b, n):
                k, half = UNITS[n]
                if half == 0:
                    turn = b if k < 2 else 0
                    pe.wait_ge(gu_hi_done[k], turn + 1)
                    pe.wait_ge(gu_lo_done[k], turn + 1)
                wait(pe, hid_done, b * NU + n - 1)
                cols = bass.ds(b * S, S)
                for dst, base in ((g_bank[n % 2], 0), (u_bank[n % 2], F)):
                    for j in (0, 1):
                        a = base + (2 * half + j) * 128
                        o = dst[:, j * S:(j + 1) * S]
                        pe.matmul(o, gu_hi[k][:, a:a + 128], xt_hi[:, cols], start=True, stop=False)
                        pe.matmul(o, gu_hi[k][:, a:a + 128], xt_lo[:, cols], start=False, stop=False)
                        last = pe.matmul(o, gu_lo[k][:, a:a + 128], xt_hi[:, cols], start=False, stop=True)
                last.then_inc(gu_mm, 1)

            def down_proj(b, n):
                k, half = UNITS[n]
                pe.wait_ge(hid_done, b * NU + n + 1)
                if half == 0:
                    turn = b if k < 2 else 0
                    pe.wait_ge(down_in[k], 16 * (turn + 1))
                if n == 0:
                    wait(pe, s["y_read"], b)
                for j in (0, 1):
                    ch = 2 * half + j
                    last = pe.matmul(y_bank[:, 0:S], down[k][:, ch * 128:(ch + 1) * 128], hid[:, n % 3, j * S:(j + 1) * S],
                                     start=(n == 0 and j == 0), stop=(n == NU - 1 and j == 1))
                last.then_inc(slot_used[k] if half else down_mm, 1)


            def effective_weights():
                pe.wait_ge(const_in, 16)
                pe.wait_ge(lora_done, B)
                for j, to in ((0, x0), (1, x1)):
                    pe.matmul(to[:], const("lora_a"), lora_scaled[:, 4 * j:4 * j + 4, :], start=True, stop=True)\
                        .then_inc(eff_mm, 1)

            def route_count(r):
                a, b = ROUTES[r]
                pe.wait_ge(rr_onehot, r + 1)
                pe.matmul(y_bank[:, a * E:b * E], earlier_b[:], onehot_b[:, a * E:b * E], start=True, stop=True)
                pe.matmul(y_bank[:, (TT + a) * E:(TT + b) * E], ones_b[:], onehot_b[:, a * E:b * E],
                          start=True, stop=True).then_inc(count_mm, 1)

            def step(n):
                if has(n, 0):
                    if isinstance(n, int) and n < 2:
                        pe.wait_ge(x_hi_done, n + 1)
                        pe.wait_ge(x_lo_done, n + 1)
                    gate_up(n, 0)
                if has(n, 3):
                    pe.wait_ge(s["rope_read"], 2 * min(n - 1, B) if isinstance(n, int) else 2 * (n - 1))
                    wait(pe, s["logit_read"], n - 3)
                    pe.wait_ge(s["tok_done"], n - 2)
                    for j in (0, 1):
                        last = pe.transpose(x0[:, j * 128:(j + 1) * 128], mixed_tok[:, j, :], const("ident"))
                    last.then_inc(s["tokt_mm"], 1)
                if has(n, 1):
                    down_proj(n - 1, NU - 2)
                if has(n, 0):
                    gate_up(n, 1)
                if has(n, 3):
                    pe.wait_ge(s["tokt_read"], n - 2)
                    pe.matmul(x1[:, 0:S], const("wout"), mixed_t[:], start=True, stop=True).then_inc(s["x1_mm"], 1)
                if isinstance(n, int) and n == B + 2:
                    route_count(1)
                if has(n, 1):
                    down_proj(n - 1, NU - 1)
                if isinstance(n, int) and n == 1:
                    effective_weights()
                if has(n, 0):
                    gate_up(n, 2)
                if has(n, 3):
                    pe.wait_ge(w_now_done, n - 2)
                    pe.wait_ge(s["x1_made"], n - 2)
                    pe.matmul(x0[:, 0:S], w_now[:], x1_t[:], start=True, stop=True).then_inc(s["t_mm"], 1)
                if has(n, 0):
                    gate_up(n, 3)
                if has(n, 3):
                    pe.wait_ge(s["t_read"], n - 2)
                    for j in (0, 1):
                        pe.transpose(x1[:, j * 2 * D:j * 2 * D + D], t_t[:, j * 128:(j + 1) * 128], const("ident"))
                        last = pe.transpose(x1[:, j * 2 * D + D:j * 2 * D + 2 * D], x1_t[:, j * 128:(j + 1) * 128], const("ident"))
                    last.then_inc(s["row_mm"], 1)
                if has(n, 0):
                    down_proj(n, 0)
                if has(n, 1):
                    if isinstance(n, int) and n == 1:
                        pe.wait_ge(eff_done, 2)
                        pe.wait_ge(ones_set, 4)
                        pe.wait_ge(bias_placed, 16)
                    pe.wait_ge(s["y_read"], n)
                    wait(pe, s["v_read"], n - 1)
                    pe.matmul(x2[0:LAT, 0:S], const("wdown"), y[:], start=True, stop=True).then_inc(s["lat_mm"], 1)
                    wait(pe, s["rope_read"], 2 * (n - 1))
                    if has(n, 3):
                        pe.wait_ge(s["row_read"], n - 2)
                    for i, (to, w) in enumerate(((x0, "wq"), (x1, "wq_swap"))):
                        pe.matmul(to[:], ones_b[0:3, :], bias_rows[:, 4 * D * i:4 * D * (i + 1)], start=True, stop=False,
                                  skip_group_check=True)
                        for j in (0, 1):
                            last = pe.matmul(to[:, j * 2 * D:j * 2 * D + D], y[:, j * 128:(j + 1) * 128], const(w),
                                             start=False, stop=False, skip_group_check=True)
                    last.then_inc(s["q_mm"], 1)
                    pe.wait_ge(s["lat_read"], n)
                    for to, w in ((x0, "wk"), (x1, "wk_swap")):
                        for j in (0, 1):
                            last = pe.matmul(to[:, j * 2 * D + D:j * 2 * D + 2 * D], lat[:, j * 128:(j + 1) * 128],
                                             const(w, LAT + 1), start=False, stop=True, skip_group_check=True)
                    last.then_inc(s["k_mm"], 1)
                    for j in (0, 1):
                        last = pe.matmul(x2[:, j * D:(j + 1) * D], lat[:, j * 128:(j + 1) * 128], const("wv", LAT + 1),
                                         start=True, stop=True)
                    last.then_inc(s["v_mm"], 1)
                if has(n, 0):
                    down_proj(n, 1)
                    down_proj(n, 2)
                if has(n, 3):
                    pe.wait_ge(s["rope_read"], 2 * min(n, B) if isinstance(n, int) else 2 * n)
                    for j in (0, 1):
                        last = pe.matmul(x0[:, j * E:(j + 1) * E], t_t[:, j * 128:(j + 1) * 128], const("switch_w"),
                                         start=True, stop=True)
                    last.then_inc(s["logit_mm"], 1)
                if has(n, 0):
                    gate_up(n, 4)
                if isinstance(n, int) and n == B + 1:
                    pe.wait_ge(s["y_read"], B)
                    route_count(0)
                if has(n, 0):
                    gate_up(n, 5)
                    down_proj(n, 3)

            pipeline(pe, step)
            route_count(2)

            def slots_t(i, o):
                t, q = at(i, o), o % RING
                wait(pe, st_done, t - 1)
                pe.wait_ge(row_in[q], fills(i, o))
                pe.transpose(st_bank[q % 2][:, 0:128], srow[q][:, 0:D], const("ident")).then_inc(st_mm, 1)

            def ffn_h(i, o):
                t, q = at(i, o), o % RING
                pe.wait_ge(hot_done, t + 1)
                wait(pe, h_done, t - 1)
                pe.wait_ge(st_done, t + 1)
                for k in range(FC):
                    last = pe.matmul(h_bank[q % 2][:, k * 128:(k + 1) * 128], hot[q][:, k * 128:(k + 1) * 128], st[q % 2],
                                     start=True, stop=True)
                last.then_inc(h_mm, 1)

            def ffn_y(i, o):
                t, q = at(i, o), o % RING
                e = pe.value_load(owner[0:1, bass.ds(t, 1)], min_val=0, max_val=E - 1)
                wait(pe, y1_done, t - 1)
                pe.wait_ge(h_done, t + 1)
                w2 = fw[:, bass.ds(e, 1), HOT_W:].rearrange("p a w -> p (a w)")
                for k in range(FC):
                    last = pe.matmul(fy_bank[q % 2][:, 0:D], fh[q % 2][:, k, :], w2[:, k * D:(k + 1) * D],
                                     start=(k == 0), stop=(k == FC - 1))
                last.then_inc(fy_mm, 1)

            def ffn_tile(i, o):
                if not (isinstance(i, int) and o < 2):
                    ffn_h(i, o - 2)
                if not (isinstance(i, int) and o < 3):
                    ffn_y(i, o - 3)
                if not (isinstance(i, int) and o >= SLOT_TILES):
                    slots_t(i, o)

            pe.wait_ge(rr_owner, 2)
            pe.wait_ge(ffn_in, 16 * E)
            tiles(pe, LEAD, SLOT_TILES, ffn_tile)
            ffn_tile(0, SLOT_TILES)
            ffn_tile(0, SLOT_TILES + 1)
            ffn_y(0, SLOT_TILES - 1)

        @block.vector
        def _(dve):
            done = [0]

            def chain(ins):
                done[0] += 1
                ins.then_inc(rt, 1)
                dve.wait_ge(rt, done[0])

            dve.wait_ge(cond_in, 16)
            chain(nc.vector.reduce_max(r_max[:], cb[:], AX))
            chain(nc.vector.tensor_tensor(r_exp[:], cb[:], r_max[:].unsqueeze(2).broadcast_to([128, B, E]), ALU.subtract))
            dve.wait_ge(r_expd, 1)
            chain(nc.vector.reduce_sum(r_sum[:], r_exp[:], AX))
            chain(nc.vector.reciprocal(r_sum[:], r_sum[:]))
            chain(nc.vector.tensor_tensor(r_prob[:], r_exp[:], r_sum[:].unsqueeze(2).broadcast_to([128, B, E]), ALU.mult))
            for b in range(B):
                ins = nc.vector.max(r_top[:, b, :], r_prob[:, b, :])
            chain(ins)
            for b in range(B):
                ins = nc.vector.max_index(chosen[:, b, :], r_top[:, b, :], r_prob[:, b, :])
            ins.then_inc(chosen_done, 1)
            chain(nc.vector.reduce_sum(r_norm[:], r_top[:, :, 0:TOP_K], AX))
            chain(nc.vector.reciprocal(r_norm[:], r_norm[:]))
            chain(nc.vector.tensor_tensor(r_w[:], r_top[:, :, 0:TOP_K], r_norm[:].unsqueeze(2).broadcast_to([128, B, TOP_K]),
                                          ALU.mult))
            chain(nc.vector.tensor_scalar(r_part[:], r_w[:], 1.0 - 1.0 / MOE_LAYERS, None, ALU.mult))
            chain(nc.vector.scalar_tensor_tensor(weight[:, :, 0:TOP_K], r_w[:], 1.0 / MOE_LAYERS, r_part[:], ALU.mult, ALU.add))
            nc.vector.memset(weight[:, :, TOP_K:TOP_K + 1], 1.0).then_inc(weight_done, 1)
            dve.wait_ge(weight_done, 1)

            def split_x(i, a, end):
                dve.wait_ge(x_in[i], 16)
                nc.vector.tensor_copy(xt_hi[:, a:end], xt[:, a:end]).then_inc(x_hi_done, 1)
                dve.wait_ge(x_hi_done, i + 1)
                nc.vector.tensor_tensor(xt_lo[:, a:end], xt[:, a:end], xt_hi[:, a:end].bitcast(F32), ALU.subtract)\
                    .then_inc(x_lo_done, 1)

            weights = weight[:].rearrange("p b k -> p (b k)")

            def unit(b, n):
                k, half = UNITS[n]
                dve.wait_ge(gelu_done, b * NU + n + 1)
                if half == 0:
                    pk, turn = UNITS[(n - 3) % NU][0], (b if n >= 3 else b - 1)
                    wait(dve, slot_used[pk], turn + 1)
                else:
                    wait(dve, down_mm, b * (NU // 2) + (n - 3) // 2 + 1)
                nc.vector.scalar_tensor_tensor(hid[:, n % 3, :], u_bank[n % 2], weights[:, bass.ds(b * (TOP_K + 1) + k, 1)],
                                               gelu[:, n % 2, :], ALU.mult, ALU.mult).then_inc(hid_done, 1)


            def bias_parts():
                dve.wait_ge(bias_in, 16)
                nc.vector.tensor_copy(bias_split[:, 0, :], bias_in_f[:]).then_inc(bias_done, 1)
                dve.wait_ge(bias_done, 1)
                chain(nc.vector.tensor_tensor(bias_rest[:], bias_in_f[:], bias_split[:, 0, :], ALU.subtract))
                nc.vector.tensor_copy(bias_split[:, 1, :], bias_rest[:]).then_inc(bias_done, 1)
                dve.wait_ge(bias_done, 2)
                nc.vector.tensor_tensor(bias_split[:, 2, :], bias_rest[:], bias_split[:, 1, :], ALU.subtract)\
                    .then_inc(bias_done, 1)

            def lora_weights():
                dve.wait_ge(const_in, 16)
                for b in range(B):
                    cond_b = const("cond_rows")[:, b:b + 1]
                    nc.vector.tensor_scalar(lora_scaled[:, b, :], const("lora_b"), cond_b, 2.0, ALU.mult, ALU.mult)\
                        .then_inc(lora_done, 1)

            def effective_sum():
                for j, of in ((0, x0), (1, x1)):
                    dve.wait_ge(eff_mm, j + 1)
                    nc.vector.tensor_tensor(w_eff[:, 4 * j:4 * j + 4, :], of[:].rearrange("p (b o) -> p b o", b=4),
                                            const("wbase").unsqueeze(1).broadcast_to([128, 4, D]), ALU.add).then_inc(eff_done, 1)
                dve.wait_ge(eff_done, 2)

            split_x(0, 0, S)

            steps = [0]

            def link(ins):
                steps[0] += 1
                ins.then_inc(rr, 1)
                dve.wait_ge(rr, steps[0])

            def over_experts(ap, n):
                return ap.unsqueeze(2).broadcast_to([128, n, E])

            def route_sub(r):
                a, b = ROUTES[r]
                dve.wait_ge(s["logit_read"], b // 2)
                link(nc.vector.reduce_max(l_max[:, a:b], logit[:, a:b, :], AX))
                nc.vector.tensor_tensor(l_exp[:, a:b, :], logit[:, a:b, :], over_experts(l_max[:, a:b], b - a), ALU.subtract)\
                    .then_inc(rr_sub, 1)

            def route_onehot(r):
                a, b = ROUTES[r]
                n = b - a
                dve.wait_ge(rr_exp, r + 1)
                link(nc.vector.scalar_tensor_tensor(l_eq[:, a:b, :], l_exp[:, a:b, :], 1.0,
                                                    const("falling").unsqueeze(1).broadcast_to([128, n, E]), ALU.is_ge, ALU.mult))
                link(nc.vector.reduce_max(l_first[:, a:b], l_eq[:, a:b, :], AX))
                link(nc.vector.tensor_tensor(onehot[:, a:b, :], l_eq[:, a:b, :], over_experts(l_first[:, a:b], n), ALU.is_equal))
                nc.vector.tensor_copy(onehot_b[:, a * E:b * E], onehot[:, a:b, :].rearrange("p t e -> p (t e)"))\
                    .then_inc(rr_onehot, 1)
                link(nc.vector.reduce_sum(l_sum[:, a:b], l_exp[:, a:b, :], AX))
                nc.vector.reciprocal(rows[:, a:b, PROB], l_sum[:, a:b]).then_inc(rr_cols, 1)

            def route_slots(r):
                a, b = ROUTES[r]
                n = b - a
                dve.wait_ge(count_mm, r + 1)
                link(nc.vector.tensor_copy(total[:, a:b, :],
                                           y_bank[:, (TT + a) * E:(TT + b) * E].rearrange("p (t e) -> p t e", e=E)))
                src, k, shift = total, 0, 1
                while shift < n:
                    dst = scan[k % 2]
                    nc.vector.tensor_copy(dst[:, a:a + shift, :], src[:, a:a + shift, :])
                    link(nc.vector.tensor_tensor(dst[:, a + shift:b, :], src[:, a + shift:b, :], src[:, a:b - shift, :], ALU.add))
                    src, k, shift = dst, k + 1, 2 * shift
                nc.vector.tensor_tensor(taken[:, r + 1, :], taken[:, r, :], src[:, b - 1, :], ALU.add).then_inc(rr_taken_f, 1)
                link(nc.vector.tensor_tensor(place[:, a:b, :], src[:, a:b, :], total[:, a:b, :], ALU.subtract))
                link(nc.vector.tensor_tensor(place[:, a:b, :], y_bank[:, a * E:b * E].rearrange("p (t e) -> p t e", e=E),
                                             place[:, a:b, :], ALU.add))
                link(nc.vector.tensor_tensor(place[:, a:b, :], place[:, a:b, :],
                                             taken[:, r, :].unsqueeze(1).broadcast_to([128, n, E]), ALU.add))
                link(nc.vector.tensor_tensor(place[:, a:b, :], place[:, a:b, :], onehot[:, a:b, :], ALU.mult))
                link(nc.vector.reduce_sum(slot_f[:, a:b], place[:, a:b, :], AX))
                nc.vector.tensor_copy(slot[:, a:b], slot_f[:, a:b]).then_inc(rr_slot, 1)

            def step(n):
                if has(n, 2):
                    less_max(n - 1, 0)
                    qk_sum(n - 1, 1)
                if has(n, 0):
                    unit(n, 0)
                if has(n, 2):
                    less_max(n - 1, 1)
                if isinstance(n, int) and n == B + 1:
                    nc.vector.tensor_copy(earlier_b[:], const("earlier_row"))
                    nc.vector.tensor_copy(taken[:, 0, :], const("region")).then_inc(rr_taken_f, 1)
                    dve.wait_ge(ids_in, 16)
                    nc.vector.tensor_copy(rows[:, :, IDX].bitcast(I32), ids[:]).then_inc(rr_cols, 1)
                    route_sub(0)
                if has(n, 3):
                    nc.vector.tensor_copy(w_now[:], w_eff[:].rearrange("p b o -> p (b o)")[:, bass.ds((n - 3) * D, D)])\
                        .then_inc(w_now_done, 1)
                    dve.wait_ge(s["x1_mm"], n - 2)
                    nc.vector.scalar_tensor_tensor(x1_t[:], x1[:, 0:S], const("bout"), xt[:, bass.ds((n - 3) * S, S)],
                                                   ALU.add, ALU.add).then_inc(s["x1_made"], 1)
                if isinstance(n, int) and n == B + 2:
                    dve.wait_ge(rr_taken_f, 2)
                    route_slots(1)
                if has(n, 0):
                    unit(n, 1)
                if isinstance(n, int) and n == 0:
                    split_x(1, S, T)
                if has(n, 2):
                    for tile in (0, 1):
                        dve.wait_ge(s[f"exp_done{tile}"], n - 1)
                    nc.vector.reduce_sum(den[:], prob[:], AX).then_inc(s["sum_done"], 1)
                if isinstance(n, int) and n == 1:
                    effective_sum()
                if has(n, 2):
                    dve.wait_ge(s["sum_done"], n - 1)
                    nc.vector.reciprocal(den[:], den[:]).then_inc(s["recip_done"], 1)
                if isinstance(n, int) and n == B + 1:
                    route_onehot(0)
                if has(n, 2) and mixes_on_dve(n):
                    dve.wait_ge(s["v_read"], n - 1)
                    dve.wait_ge(s["pv_done"], 2 * (n - 2))
                    nc.vector.tensor_tensor(pv_prod[:, 1], prob[:, 1].unsqueeze(2).broadcast_to([128, NH, DH, NH]),
                                            v[:, 1].unsqueeze(1).broadcast_to([128, NH, DH, NH]), ALU.mult)\
                        .then_inc(s["pv_prod_done1"], 1)
                if has(n, 2):
                    values_sum(n, 0)
                if has(n, 0):
                    unit(n, 2)
                    unit(n, 3)
                if isinstance(n, int) and n == 0:
                    bias_parts()
                if has(n, 1):
                    dve.wait_ge(s["k_mm"], n)
                    for i, (of, table) in enumerate(((x0, "cos"), (x1, "sin"))):
                        nc.vector.tensor_tensor(rope[:, i, :], of[:], const(table), ALU.mult).then_inc(s["rope_read"], 1)
                    dve.wait_ge(s["rope_read"], 2 * n)
                    nc.vector.tensor_tensor(qk[:].rearrange("p t j h d -> p (t j h d)"), rope[:, 0, :], rope[:, 1, :],
                                            ALU.add).then_inc(s["turned"], 1)
                    dve.wait_ge(s["turned"], n)
                    nc.vector.tensor_tensor(qk_prod[:, 0], qk[:, 0, 0].unsqueeze(2).broadcast_to([128, NH, NH, DH]),
                                            qk[:, 0, 1].unsqueeze(1).broadcast_to([128, NH, NH, DH]), ALU.mult)\
                        .then_inc(s["qk_prod_done0"], 1)
                if isinstance(n, int) and n == 0:
                    lora_weights()
                if has(n, 3):
                    dve.wait_ge(s["logit_mm"], n - 2)
                    dst = logit[:].rearrange("p t e -> p (t e)")[:, bass.ds((n - 3) * 2 * E, 2 * E)]
                    nc.vector.tensor_tensor(dst.rearrange("p (t e) -> p t e", e=E),
                                            x0[:, 0:2 * E].rearrange("p (t e) -> p t e", e=E),
                                            const("switch_b").unsqueeze(1).broadcast_to([128, 2, E]), ALU.add)\
                        .then_inc(s["logit_read"], 1)
                if has(n, 2):
                    values_sum(n, 1)
                if has(n, 0):
                    unit(n, 4)
                if has(n, 1):
                    qk_sum(n, 0)
                if has(n, 2):
                    dve.wait_ge(s["recip_done"], n - 1)
                    dve.wait_ge(s["pv_done"], 2 * (n - 1))
                    wait(dve, s["tokt_mm"], n - 2)
                    nc.vector.tensor_tensor(mixed_tok[:].rearrange("p t (h d) -> p t h d", d=DH), mixed[:],
                                            den[:].unsqueeze(3).broadcast_to([128, 2, NH, DH]), ALU.mult)\
                        .then_inc(s["tok_done"], 1)
                if isinstance(n, int) and n == B + 1:
                    dve.wait_ge(rr_taken_f, 1)
                    route_slots(0)
                    route_sub(1)
                    route_onehot(1)
                if has(n, 0):
                    unit(n, 5)

            def values_sum(n, tile):
                dve.wait_ge(s[f"pv_prod_done{tile}"], n - 1)
                nc.vector.reduce_sum(mixed[:, tile], pv_prod[:, tile], AX).then_inc(s["pv_done"], 1)

            def qk_sum(n, tile):
                dve.wait_ge(s[f"qk_prod_done{tile}"], n)
                wait(dve, s[f"exp_done{tile}"], n - 1)
                nc.vector.reduce_sum(score[:, tile], qk_prod[:, tile], AX).then_inc(s["score_done"], 1)

            def less_max(n, tile):
                dve.wait_ge(s["score_done"], 2 * n - 1 + tile)
                nc.vector.reduce_max(s_max[:, tile], score[:, tile], AX).then_inc(s["max_done"], 1)
                dve.wait_ge(s["max_done"], 2 * n - 1 + tile)
                nc.vector.tensor_tensor(score[:, tile], score[:, tile],
                                        s_max[:, tile].unsqueeze(2).broadcast_to([128, NH, NH]), ALU.subtract)\
                    .then_inc(s[f"sub_done{tile}"], 1)

            pipeline(dve, step)
            route_sub(2)
            route_onehot(2)
            dve.wait_ge(rr_taken_f, 3)
            route_slots(2)
            dve.wait_ge(rr_taken_f, 4)
            final = taken[:, len(ROUTES), :]
            nc.vector.tensor_copy(taken_u[:], final).then_inc(rr_taken, 1)
            link(nc.vector.tensor_tensor(over[:], final.unsqueeze(2).broadcast_to([128, E, TT]),
                                         const("ramp").rearrange("p (e t) -> p e t", e=E), ALU.is_gt))
            link(nc.vector.reduce_sum(n_tiles[:], over[:], AX))
            link(nc.vector.tensor_tensor(prev_tiles[:], n_tiles[:].unsqueeze(1).broadcast_to([128, E, E]),
                                         const("up_to").rearrange("p (a b) -> p a b", a=E), ALU.mult))
            link(nc.vector.reduce_sum(end_tile[:], prev_tiles[:], AX))
            link(nc.vector.tensor_scalar(skip[:], n_tiles[:], -128.0, float(REGION), ALU.mult, ALU.add))
            link(nc.vector.tensor_tensor(ended[:], end_tile[:].unsqueeze(1).broadcast_to([128, OWNED, E]),
                                         const("slot_tile").unsqueeze(2).broadcast_to([128, OWNED, E]), ALU.is_le))
            link(nc.vector.tensor_tensor(skipped[:], ended[:], skip[:].unsqueeze(1).broadcast_to([128, OWNED, E]), ALU.mult))
            link(nc.vector.reduce_sum(source_f[:], skipped[:], AX))
            link(nc.vector.scalar_tensor_tensor(source_f[:], const("slot_tile"), 128.0, source_f[:], ALU.mult, ALU.add))
            nc.vector.tensor_scalar(source[:], source_f[:], float(E * REGION), None, ALU.min).then_inc(rr_owner, 1)
            link(nc.vector.reduce_sum(owner_f[:], ended[:], AX))
            nc.vector.tensor_scalar(owner[:], owner_f[:], float(E - 1), None, ALU.min).then_inc(rr_owner, 1)


            def ffn_hot(i, o):
                t, q = at(i, o), o % RING
                e = dve.value_load(owner[0:1, bass.ds(t, 1)], min_val=0, max_val=E - 1)
                nc.vector.tensor_copy(hot[q], fw[:, bass.ds(e, 1), 0:HOT_W].rearrange("p a w -> p (a w)"))\
                    .then_inc(hot_done, 1)

            def ffn_st(i, o):
                t, q = at(i, o), o % RING
                wait(dve, h_mm, t - 1)
                dve.wait_ge(st_mm, t + 1)
                nc.vector.tensor_copy(st[q % 2], st_bank[q % 2][:, 0:128]).then_inc(st_done, 1)

            def ffn_y1(i, o):
                t, q = at(i, o), o % RING
                wait(dve, z_done, t - 1)
                dve.wait_ge(fy_mm, t + 1)
                nc.vector.tensor_tensor(y1[q % 2], fy_bank[q % 2][:, 0:D], hot[q][:, F + FC:], ALU.add).then_inc(y1_done, 1)

            def ffn_z(i, o):
                t, q = at(i, o), o % RING
                wait(dve, yo_done, t - 1)
                dve.wait_ge(y1_done, t + 1)
                nc.vector.tensor_scalar(z[q % 2], y1[q % 2], srow[q][:, PROB:PROB + 1], None, ALU.mult).then_inc(z_done, 1)

            def ffn_tile(i, o):
                if not (isinstance(i, int) and o < 3):
                    ffn_y1(i, o - 3)
                if not (isinstance(i, int) and o >= SLOT_TILES):
                    ffn_st(i, o)
                if not (isinstance(i, int) and o < 3):
                    ffn_z(i, o - 3)
                if not (isinstance(i, int) and o >= SLOT_TILES):
                    ffn_hot(i, o + HOT_AHEAD)

            dve.wait_ge(ffn_in, 16 * E)
            dve.wait_ge(rr_owner, 2)
            for t in range(HOT_AHEAD):
                ffn_hot(0, t)
            tiles(dve, LEAD, SLOT_TILES, ffn_tile)
            for t in range(SLOT_TILES, SLOT_TILES + 3):
                ffn_tile(0, t)


def kernel(**inputs):
    import numpy as np
    import concourse.bacc as bacc
    from concourse.bass_utils import run_bass_kernel_spmd

    a = {k: np.asarray(val) for k, val in inputs.items()}
    x_t = np.ascontiguousarray(a["x"].reshape(T, D).T)

    def chunked(w):
        return w.reshape(*w.shape[:-2], FC, 128, D).swapaxes(-3, -2).reshape(*w.shape[:-2], 128, FC * D)

    skill = np.concatenate([a["L0_cond_skill_gate"], a["L0_cond_skill_up"], chunked(a["L0_cond_skill_down"])], axis=2)
    shared = np.concatenate([a["L0_cond_shared_gate"], a["L0_cond_shared_up"], chunked(a["L0_cond_shared_down"])], axis=1)
    experts = np.ascontiguousarray(np.concatenate([skill, shared[None]], axis=0))
    ffn = np.ascontiguousarray(np.concatenate([
        a["L0_ffn_w1"], a["L0_ffn_b1"].reshape(E, FC, 128).swapaxes(1, 2),
        np.broadcast_to(a["L0_ffn_b2"][:, None, :], (E, 128, D)), chunked(a["L0_ffn_w2"])], axis=2))
    cond = np.ascontiguousarray(np.broadcast_to(a["cond_8"].reshape(1, B * E), (128, B * E)))

    pos = np.arange(S, dtype=np.float32)
    freq = (1.0 / np.float32(10000.0) ** (np.arange(0, DH, 2, dtype=np.float32) / DH)).astype(np.float32)
    angle = (pos[:, None] * freq[None, :]).astype(np.float32)
    half = DH // 2
    feature = np.arange(D)
    sign = np.where(feature % DH < half, -1, 1).astype(np.float32)
    cos = np.tile(np.cos(angle).astype(np.float32)[:, feature % half].reshape(2, 128, 1, D), (1, 1, 2, 1))
    sin = np.tile((np.sin(angle).astype(np.float32)[:, feature % half] * sign).reshape(2, 128, 1, D), (1, 1, 2, 1))
    cos, sin = (a_.transpose(1, 0, 2, 3).reshape(128, 4 * D) for a_ in (cos, sin))
    swap = (feature // DH) * DH + (feature % DH + half) % DH
    k_cols = (feature // DH) * 2 * DH + feature % DH
    up = np.concatenate([a["L0_attn_Wup"], a["L0_attn_bup"][None]], axis=0)
    order = np.arange(128)
    r = a["L0_cond2_As"].shape[1]
    full = {
        "switch_b": np.broadcast_to(a["L0_ffn_switch_b"][None], (128, E)),
        "cond_rows": np.repeat(a["cond_8"].T, r, axis=0),
        "wq": a["L0_attn_Wq"], "wq_swap": a["L0_attn_Wq"][:, swap],
        "wk": up[:, k_cols], "wk_swap": up[:, k_cols[swap]], "wv": up[:, k_cols + DH],
        "wdown": a["L0_attn_Wdown"],
        "bdown": a["L0_attn_bdown"][:, None], "wout": a["L0_attn_Wout"], "bout": a["L0_attn_bout"][:, None],
        "wbase": a["L0_cond2_W_base"].T, "bbase": a["L0_cond2_b_base"][:, None],
        "lora_a": a["L0_cond2_As"].reshape(E * r, D), "lora_b": a["L0_cond2_Bs"].swapaxes(1, 2).reshape(E * r, D),
        "switch_w": a["L0_ffn_switch_w"], "cos": cos, "sin": sin, "ident": np.eye(128, dtype=np.float32),
        "earlier_row": (order[:, None] < order[None, :]).astype(np.float32),
        "falling": np.broadcast_to(np.arange(E, 0, -1, dtype=np.float32), (128, E)),
        "region": np.broadcast_to(REGION * np.arange(E, dtype=np.float32), (128, E)),
        "ramp": np.broadcast_to((REGION * np.arange(E)[:, None] + 128 * np.arange(TT)[None]).astype(np.float32)
                                .reshape(1, E * TT), (128, E * TT)),
        "up_to": np.broadcast_to((np.arange(E)[None, :] <= np.arange(E)[:, None]).astype(np.float32).reshape(1, E * E),
                                  (128, E * E)),
        "slot_tile": np.broadcast_to(np.arange(OWNED, dtype=np.float32), (128, OWNED)),
    }
    consts = np.zeros((128, CONST_W), np.float32)
    for name, (at, width) in AT.items():
        consts[:full[name].shape[0], at:at + width] = full[name]
    query_bias = np.zeros((2, 2, 2, D), np.float32)
    query_bias[0, :, 0], query_bias[1, :, 0] = a["L0_attn_bq"], a["L0_attn_bq"][swap]
    query_bias = query_bias.reshape(8, D)
    token_ids = np.ascontiguousarray(np.arange(T, dtype=np.int32).reshape(TT, 128).T)

    arrays = {"in_x_t": x_t, "in_cond": cond, "in_experts": experts, "in_ffn": ffn, "in_consts": consts, "in_query_bias": query_bias,
              "in_token_ids": token_ids}
    nc = bacc.Bacc("TRN2", target_bir_lowering=False, num_devices=1)
    args = [nc.dram_tensor(name, v.shape, mybir.dt.from_np(v.dtype), kind="ExternalInput").ap() for name, v in arrays.items()]
    out = nc.dram_tensor("out", (T, D), F32, kind="ExternalOutput").ap()
    adaln_program(nc, *args, out)
    r = run_bass_kernel_spmd(nc, [arrays], core_ids=[0])
    return r.results[0]["out"].reshape(B, S, D)
```
